# Optimizing a Trainium2 kernel written in Bass

```python
import numpy as np
import jax
import jax.numpy as jnp

def _softmax(x, axis=-1):
    return jax.nn.softmax(x, axis=axis)

def _gelu(x):
    return jax.nn.gelu(x, approximate=True)

def _silu(x):
    return jax.nn.silu(x)

def _sigmoid(x):
    return jax.nn.sigmoid(x)

def _layernorm(x, axis=-1, eps=1e-05):
    m = jnp.mean(x, axis=axis, keepdims=True)
    v = jnp.var(x, axis=axis, keepdims=True)
    return (x - m) / jnp.sqrt(v + eps)

def _scatter_add(tgt, idx, src, axis=0):
    return tgt.at[idx].add(src)

def _segment_sum(src, seg, n):
    return jax.ops.segment_sum(src, seg, n)
kernel_name = 'mk_audio_tower_d1_tok_aud1d768_r4_e2d1c7'

def setup_inputs(seed: int=0):
    np.random.seed(seed)
    _w = jnp.asarray

    def _rec_inputs():
        import jax
        import jax.numpy as jnp
        _rk = jax.random.key(seed)
        x = -6.41493e-05 + 1.00002 * jax.random.normal(jax.random.fold_in(_rk, 1), (64, 20000), jnp.float32)
        return x
    x = _rec_inputs()

    def _L0_tok_setup():
        import jax, jax.numpy as jnp
        import numpy as np
        import math
        SR = 4000
        FRAME_LEN = 100
        FRAME_STEP = 160
        N_FILTERS = 40
        N_MFCC = 13
        EMBED = 192
        BATCH = 64
        AUDIO_LEN = 40000
        N_FFT_BINS = FRAME_LEN // 2 + 1

        def _mel_filterbank():
            low_mel = 2595.0 * math.log10(1.0 + 0.0 / 700.0)
            high_mel = 2595.0 * math.log10(1.0 + SR // 2 / 700.0)
            mel_points = np.linspace(low_mel, high_mel, N_FILTERS + 2)
            hz_points = 700.0 * (10.0 ** (mel_points / 2595.0) - 1.0)
            bin_points = np.floor((FRAME_LEN + 1) * hz_points / SR)
            filt = np.zeros((N_FILTERS, N_FFT_BINS), dtype=np.float32)
            for i in range(1, N_FILTERS + 1):
                l, c, r = (bin_points[i - 1], bin_points[i], bin_points[i + 1])
                for j in range(int(l), int(c)):
                    filt[i - 1, j] = (j - l) / (c - l)
                for j in range(int(c), int(r)):
                    filt[i - 1, j] = (r - j) / (r - c)
            return jnp.asarray(filt)

        def _dct_matrix():
            k = np.arange(N_MFCC)[:, None]
            j = np.arange(N_FILTERS)[None, :]
            m = np.cos(np.pi * k * (2 * j + 1) / (2 * N_FILTERS)) * math.sqrt(2.0 / N_FILTERS)
            return jnp.asarray(m.astype(np.float32))
        key = jax.random.key(seed)
        kx, kw = jax.random.split(key)
        x = jax.random.normal(kx, (BATCH, AUDIO_LEN), dtype=jnp.float32)
        bound = 1.0 / math.sqrt(N_MFCC)
        w_proj = jax.random.uniform(kw, (N_MFCC, EMBED), minval=-bound, maxval=bound, dtype=jnp.float32)
        b_proj = jnp.zeros((EMBED,), dtype=jnp.float32)
        return {'x': x, 'mel_filters': _mel_filterbank(), 'dct': _dct_matrix(), 'w_proj': w_proj, 'b_proj': b_proj}
    _L0_tok_all = _L0_tok_setup()
    _L0_tok_in = {k: v for k, v in _L0_tok_all.items() if k in ('mel_filters', 'dct', 'w_proj', 'b_proj')}
    del _L0_tok_all

    def _L0_attn_setup():
        import jax, jax.numpy as jnp
        import numpy as np
        DIM = 192
        HEADS = 12
        DH = DIM // HEADS
        M = 64
        EPS = 0.0001

        def softmax_kernel(data, proj, is_query):
            data_normalizer = data.shape[-1] ** (-0.25)
            ratio = proj.shape[0] ** (-0.5)
            data_dash = jnp.einsum('bhsd,md->bhsm', data_normalizer * data, proj)
            diag = 0.5 * data_normalizer ** 2 * jnp.sum(data * data, axis=-1, keepdims=True)
            if is_query:
                stab = jnp.max(data_dash, axis=-1, keepdims=True)
            else:
                stab = jnp.max(data_dash, axis=(-2, -1), keepdims=True)
            stab = jax.lax.stop_gradient(stab)
            return ratio * (jnp.exp(data_dash - diag - stab) + EPS)
        key = jax.random.key(seed)
        kx, kq, kk, kv, ko, kp = jax.random.split(key, 6)
        B, S = (8, 1024)
        w_scale = DIM ** (-0.5)
        return {'x': jax.random.normal(kx, (B, S, DIM), jnp.float32), 'Wq': jax.random.normal(kq, (DIM, DIM), jnp.float32) * w_scale, 'Wk': jax.random.normal(kk, (DIM, DIM), jnp.float32) * w_scale, 'Wv': jax.random.normal(kv, (DIM, DIM), jnp.float32) * w_scale, 'Wo': jax.random.normal(ko, (DIM, DIM), jnp.float32) * w_scale, 'proj': jax.random.normal(kp, (M, DH), jnp.float32)}
    _L0_attn_all = _L0_attn_setup()
    _L0_attn_in = {k: v for k, v in _L0_attn_all.items() if k in ('Wq', 'Wk', 'Wv', 'Wo', 'proj')}
    del _L0_attn_all

    def _L0_ffn_setup():
        import jax, jax.numpy as jnp
        import numpy as np
        import math
        B, T, C = (8, 512, 192)
        E = 3
        HD = C // E
        TOPK = 2
        NGLOB = 4

        def _masked_softmax(att, mask):
            att = jnp.where(mask, -jnp.inf, att)
            return jax.nn.softmax(att, axis=-1)
        key = jax.random.key(seed)
        ks = jax.random.split(key, 16)
        s = 0.02
        return {'x': jax.random.normal(ks[0], (B, T, C), jnp.float32), 'Wqk': jax.random.normal(ks[1], (C, 2 * C), jnp.float32) * s, 'bqk': jnp.zeros((2 * C,), jnp.float32), 'Wv': jax.random.normal(ks[2], (E, C, HD), jnp.float32) * s, 'bv': jnp.zeros((E, HD), jnp.float32), 'conv_w': jax.random.normal(ks[3], (HD, 1, 3), jnp.float32) * s, 'conv_b': jnp.zeros((HD,), jnp.float32), 'glob': jax.random.normal(ks[4], (NGLOB, HD), jnp.float32) * 0.02, 'pos_bias': jnp.zeros((64, 64), jnp.float32), 'Wg1': jax.random.normal(ks[5], (C, 32), jnp.float32) * s, 'bg1': jnp.zeros((32,), jnp.float32), 'Wg2': jax.random.normal(ks[6], (32, E), jnp.float32) * s, 'bg2': jnp.zeros((E,), jnp.float32), 'Wp': jax.random.normal(ks[7], (C, C), jnp.float32) * s, 'bp': jnp.zeros((C,), jnp.float32)}
    _L0_ffn_all = _L0_ffn_setup()
    _L0_ffn_in = {k: v for k, v in _L0_ffn_all.items() if k in ('Wqk', 'bqk', 'Wv', 'bv', 'conv_w', 'conv_b', 'glob', 'pos_bias', 'Wg1', 'bg1', 'Wg2', 'bg2', 'Wp', 'bp')}
    del _L0_ffn_all
    return {'x': x, 'L0_tok_mel_filters': _L0_tok_in['mel_filters'], 'L0_tok_dct': _L0_tok_in['dct'], 'L0_tok_w_proj': _L0_tok_in['w_proj'], 'L0_tok_b_proj': _L0_tok_in['b_proj'], 'L0_attn_Wq': _L0_attn_in['Wq'], 'L0_attn_Wk': _L0_attn_in['Wk'], 'L0_attn_Wv': _L0_attn_in['Wv'], 'L0_attn_Wo': _L0_attn_in['Wo'], 'L0_attn_proj': _L0_attn_in['proj'], 'L0_ffn_Wqk': _L0_ffn_in['Wqk'], 'L0_ffn_bqk': _L0_ffn_in['bqk'], 'L0_ffn_Wv': _L0_ffn_in['Wv'], 'L0_ffn_bv': _L0_ffn_in['bv'], 'L0_ffn_conv_w': _L0_ffn_in['conv_w'], 'L0_ffn_conv_b': _L0_ffn_in['conv_b'], 'L0_ffn_glob': _L0_ffn_in['glob'], 'L0_ffn_pos_bias': _L0_ffn_in['pos_bias'], 'L0_ffn_Wg1': _L0_ffn_in['Wg1'], 'L0_ffn_bg1': _L0_ffn_in['bg1'], 'L0_ffn_Wg2': _L0_ffn_in['Wg2'], 'L0_ffn_bg2': _L0_ffn_in['bg2'], 'L0_ffn_Wp': _L0_ffn_in['Wp'], 'L0_ffn_bp': _L0_ffn_in['bp']}

def reference(x, L0_tok_mel_filters, L0_tok_dct, L0_tok_w_proj, L0_tok_b_proj, L0_attn_Wq, L0_attn_Wk, L0_attn_Wv, L0_attn_Wo, L0_attn_proj, L0_ffn_Wqk, L0_ffn_bqk, L0_ffn_Wv, L0_ffn_bv, L0_ffn_conv_w, L0_ffn_conv_b, L0_ffn_glob, L0_ffn_pos_bias, L0_ffn_Wg1, L0_ffn_bg1, L0_ffn_Wg2, L0_ffn_bg2, L0_ffn_Wp, L0_ffn_bp):
    import jax
    import jax.numpy as jnp

    def _L0_tok_ref(x, mel_filters, dct, w_proj, b_proj):
        import jax, jax.numpy as jnp
        import numpy as np
        import math
        SR = 4000
        FRAME_LEN = 100
        FRAME_STEP = 160
        N_FILTERS = 40
        N_MFCC = 13
        EMBED = 192
        BATCH = 64
        AUDIO_LEN = 40000
        N_FFT_BINS = FRAME_LEN // 2 + 1

        def _mel_filterbank():
            low_mel = 2595.0 * math.log10(1.0 + 0.0 / 700.0)
            high_mel = 2595.0 * math.log10(1.0 + SR // 2 / 700.0)
            mel_points = np.linspace(low_mel, high_mel, N_FILTERS + 2)
            hz_points = 700.0 * (10.0 ** (mel_points / 2595.0) - 1.0)
            bin_points = np.floor((FRAME_LEN + 1) * hz_points / SR)
            filt = np.zeros((N_FILTERS, N_FFT_BINS), dtype=np.float32)
            for i in range(1, N_FILTERS + 1):
                l, c, r = (bin_points[i - 1], bin_points[i], bin_points[i + 1])
                for j in range(int(l), int(c)):
                    filt[i - 1, j] = (j - l) / (c - l)
                for j in range(int(c), int(r)):
                    filt[i - 1, j] = (r - j) / (r - c)
            return jnp.asarray(filt)

        def _dct_matrix():
            k = np.arange(N_MFCC)[:, None]
            j = np.arange(N_FILTERS)[None, :]
            m = np.cos(np.pi * k * (2 * j + 1) / (2 * N_FILTERS)) * math.sqrt(2.0 / N_FILTERS)
            return jnp.asarray(m.astype(np.float32))
        B, T = x.shape
        n_frames = 1 + (T - FRAME_LEN) // FRAME_STEP
        idx = jnp.arange(n_frames)[:, None] * FRAME_STEP + jnp.arange(FRAME_LEN)[None, :]
        frames = x[:, idx]
        window = 0.54 - 0.46 * jnp.cos(2.0 * jnp.pi * jnp.arange(FRAME_LEN, dtype=jnp.float32) / (FRAME_LEN - 1))
        windowed = frames * window
        fft = jnp.fft.rfft(windowed, axis=-1)
        power = fft.real ** 2 + fft.imag ** 2
        mel_energies = jnp.einsum('bnf,mf->bnm', power, mel_filters)
        log_energies = jnp.log(mel_energies + 1e-06)
        mfcc = jnp.einsum('bnm,km->bnk', log_energies, dct)
        out = mfcc @ w_proj + b_proj
        return out

    def _L0_attn_ref(x, Wq, Wk, Wv, Wo, proj):
        import jax, jax.numpy as jnp
        import numpy as np
        DIM = 192
        HEADS = 12
        DH = DIM // HEADS
        M = 64
        EPS = 0.0001

        def softmax_kernel(data, proj, is_query):
            data_normalizer = data.shape[-1] ** (-0.25)
            ratio = proj.shape[0] ** (-0.5)
            data_dash = jnp.einsum('bhsd,md->bhsm', data_normalizer * data, proj)
            diag = 0.5 * data_normalizer ** 2 * jnp.sum(data * data, axis=-1, keepdims=True)
            if is_query:
                stab = jnp.max(data_dash, axis=-1, keepdims=True)
            else:
                stab = jnp.max(data_dash, axis=(-2, -1), keepdims=True)
            stab = jax.lax.stop_gradient(stab)
            return ratio * (jnp.exp(data_dash - diag - stab) + EPS)
        B, S, _ = x.shape

        def split_heads(t):
            return t.reshape(B, S, HEADS, DH).transpose(0, 2, 1, 3)
        q = split_heads(x @ Wq)
        k = split_heads(x @ Wk)
        v = split_heads(x @ Wv)
        qp = softmax_kernel(q, proj, is_query=True)
        kp = softmax_kernel(k, proj, is_query=False)
        k_sum = jnp.sum(kp, axis=2)
        d_inv = 1.0 / jnp.einsum('bhsm,bhm->bhs', qp, k_sum)
        ctx = jnp.einsum('bhsm,bhsd->bhmd', kp, v)
        out = jnp.einsum('bhsm,bhmd,bhs->bhsd', qp, ctx, d_inv)
        out = out.transpose(0, 2, 1, 3).reshape(B, S, DIM)
        return out @ Wo

    def _L0_ffn_ref(x, Wqk, bqk, Wv, bv, conv_w, conv_b, glob, pos_bias, Wg1, bg1, Wg2, bg2, Wp, bp):
        import jax, jax.numpy as jnp
        import numpy as np
        import math
        B, T, C = (8, 512, 192)
        E = 3
        HD = C // E
        TOPK = 2
        NGLOB = 4

        def _masked_softmax(att, mask):
            att = jnp.where(mask, -jnp.inf, att)
            return jax.nn.softmax(att, axis=-1)
        Bx, Tx, Cx = x.shape
        scale = 1.0 / math.sqrt(HD)
        gate = jax.nn.softmax(jax.nn.relu(x @ Wg1 + bg1) @ Wg2 + bg2, axis=-1)
        top_w, top_i = jax.lax.top_k(gate, TOPK)
        top_w = jax.nn.softmax(top_w, axis=-1)
        qk = x @ Wqk + bqk
        q, k = (qk[..., :Cx], qk[..., Cx:])
        q = q.reshape(Bx, Tx, E, HD)
        k = k.reshape(Bx, Tx, E, HD)
        rows = jnp.arange(Tx)[:, None]
        ys = []
        for e in range(E):
            qe = q[:, :, e]
            ke = k[:, :, e]
            ve = x @ Wv[e] + bv[e]
            if e == 0:
                qc = jnp.transpose(qe, (0, 2, 1))
                qc = jax.lax.conv_general_dilated(qc, conv_w, window_strides=(1,), padding=((1, 1),), feature_group_count=HD, dimension_numbers=('NCH', 'OIH', 'NCH'))
                qe = jnp.transpose(qc + conv_b[None, :, None], (0, 2, 1))
            elif e == 1:
                gb = jnp.broadcast_to(glob[None], (Bx, NGLOB, HD))
                ke = jnp.concatenate([ke, gb], axis=1)
                ve = jnp.concatenate([ve, gb], axis=1)
            att = jnp.einsum('btd,bsd->bts', qe, ke) * scale
            if e == 2 and Tx <= 64:
                att = att + pos_bias[:Tx, :Tx][None]
            S = att.shape[-1]
            mask = jnp.arange(S)[None, :] > rows
            att = _masked_softmax(att, mask[None])
            ys.append(jnp.einsum('bts,bsd->btd', att, ve))
        ys = jnp.stack(ys, axis=2)
        w_e = jnp.sum(jax.nn.one_hot(top_i, E, dtype=x.dtype) * top_w[..., None], axis=-2)
        combined = (ys * w_e[..., None]).reshape(Bx, Tx, Cx)
        return combined @ Wp + bp
    h = _L0_tok_ref(x, L0_tok_mel_filters, L0_tok_dct, L0_tok_w_proj, L0_tok_b_proj)
    h = h + _L0_attn_ref(_layernorm(h, axis=-1), L0_attn_Wq, L0_attn_Wk, L0_attn_Wv, L0_attn_Wo, L0_attn_proj)
    h = h + _L0_ffn_ref(_layernorm(h, axis=-1), L0_ffn_Wqk, L0_ffn_bqk, L0_ffn_Wv, L0_ffn_bv, L0_ffn_conv_w, L0_ffn_conv_b, L0_ffn_glob, L0_ffn_pos_bias, L0_ffn_Wg1, L0_ffn_bg1, L0_ffn_Wg2, L0_ffn_bg2, L0_ffn_Wp, L0_ffn_bp)
    return h

_drawn_inputs = setup_inputs


def setup_inputs(seed=0):
    import zlib

    import numpy as np

    out = dict(_drawn_inputs(seed))
    spreads = {'L0_tok_b_proj': (0.0, 0.337),
     'L0_ffn_bqk': (0.0, 2.0),
     'L0_ffn_bv': (0.0, 0.8),
     'L0_ffn_conv_b': (0.0, 0.8),
     'L0_ffn_pos_bias': (0.0, 0.1),
     'L0_ffn_bg1': (0.0, 0.8),
     'L0_ffn_bg2': (0.0, 0.8),
     'L0_ffn_bp': (0.0, 0.343)}
    factors = {'L0_attn_Wq': 64.0,
     'L0_attn_Wk': 8.0,
     'L0_attn_proj': 8.0,
     'L0_ffn_Wqk': 24.395,
     'L0_ffn_Wv': 8.0,
     'L0_ffn_conv_w': 8.0,
     'L0_ffn_Wg1': 8.0,
     'L0_ffn_Wg2': 8.0,
     'L0_ffn_Wp': 7.797}
    for name, (base, spread) in spreads.items():
        noise = np.random.default_rng([zlib.crc32(name.encode()), seed]).standard_normal(out[name].shape)
        drawn = base * np.exp(spread * noise) if base else spread * noise
        out[name] = jnp.asarray(drawn.astype(out[name].dtype))
    for name, factor in factors.items():
        out[name] = (out[name] * factor).astype(out[name].dtype)
    return out
```

```python
import itertools

import concourse.bass as bass
from concourse import mybir
from contextlib import ExitStack

BATCH, AUDIO = 64, 20000
FRAME, STEP = 100, 160
S = 1 + (AUDIO - FRAME) // STEP
NFFT = FRAME // 2 + 1
NPOW = FRAME
NMEL, NMFCC, DIM = 40, 13, 192
NY = NMFCC + 1
HW = DIM + NY
HEADS, DH, M = 12, 16, 64
HH = HEADS // 2
NE, HD = 3, 64
KT = DIM // 2
G = 4
NG = BATCH // G
LN_EPS = 1e-5
LOG_EPS = 1e-6
LN_1E4 = 9.210340371976184
NEG = -1e30

PAIRS = [(0, 0), (0, 1), (0, 2), (1, 0), (1, 1), (2, 0)]
KY = len(PAIRS) * NY
KB = 3 * HEADS
KZ = KY + KB
ZW = 2 * KZ


def audio_tower(nc, ins, out):
    fp32, bf16 = mybir.dt.float32, mybir.dt.bfloat16
    ALU, ACT, AX = mybir.AluOpType, mybir.ActivationFunctionType, mybir.AxisListType.X
    ctx = ExitStack()

    def sb(name, shape, dt=fp32):
        return ctx.enter_context(nc.sbuf_tensor(name, shape, dt))

    def sem(name):
        return ctx.enter_context(nc.semaphore(name))

    with ctx:
        dft = sb("dft", [FRAME, NPOW])
        ident = sb("ident", [128, 128])
        identb = sb("identb", [128, 128], bf16)
        eq_c = sb("eq_c", [KZ, HEADS * M])
        ek_c = sb("ek_c", [KZ, HEADS * M])
        selq = sb("selq", [KZ, 3])
        selk = sb("selk", [KZ, 3])
        blk = sb("blk", [KT, HH * NY])
        causal = sb("causal", [S, S])
        causalb = sb("causalb", [S, NE, S], bf16)
        ones = sb("ones", [128, 128])
        onesb = sb("onesb", [128, 128], bf16)
        bd = sb("bd", [128, 2])
        log_eps = sb("log_eps", [128, 1])
        neg_half = sb("neg_half", [128, G])
        mel2 = sb("mel2", [NPOW, NMEL])
        dctx = sb("dctx", [NY, NMEL + 1])
        pd = sb("pd", [NMEL + 1, HW])
        wpb = sb("wpb", [NY, DIM])
        wpc = sb("wpc", [NY, DIM])
        wrow = sb("wrow", [NY, 2])
        wpcT = sb("wpcT", [KT, 2, NY])
        wpcT6 = sb("wpcT6", [KT, 2, KY])
        wqk_a = sb("wqk_a", [KT, 2, 2 * DIM])
        wv_a = sb("wv_a", [KT, 2, DIM])
        wo_a = sb("wo_a", [KT, 2, DIM])
        projb = sb("projb", [KT, HH * M])
        a6 = sb("a6", [KT, 4, KB + KY + KB])
        avT = sb("avT", [KT, 2, HH * NY])
        w_raw = sb("w_raw", [KY, 2 * DIM], bf16)
        w_q0 = sb("w_q0", [KY, HEADS * M], bf16)
        w_qe = sb("w_qe", [KZ, HEADS * M], bf16)
        w_ke = sb("w_ke", [KZ, HEADS * M], bf16)
        w_vo = sb("w_vo", [HH * NY, 2, DIM])
        part = [sb(f"part{i}", [KZ, HH * M], bf16) for i in range(3)]
        rest = sb("rest", [KZ, HH * M])
        acc = sb("acc", [KZ, HH * M])
        f_wqk = sb("f_wqk", [KT + 1, 2, 2 * DIM])
        f_wv = sb("f_wv", [KT + 1, 2, DIM])
        f_wp = sb("f_wp", [KT + 1, 2, DIM])
        f_wg1 = sb("f_wg1", [KT + 1, 2, 32])
        f_wg2 = sb("f_wg2", [33, NE])
        f_cw = sb("f_cw", [HD, 3])
        f_cb = sb("f_cb", [HD, 1])

        h_all = sb("h_all", [S, BATCH, HW])
        zt_all = sb("zt_all", [S, BATCH, ZW], bf16)
        ysT_all = sb("ysT_all", [KY, BATCH, S], bf16)
        y_all = sb("y_all", [S, BATCH, NY])
        yk_all = sb("yk_all", [S, BATCH, 3, NY + 1], bf16)

        bank = [ctx.enter_context(nc.psum_tensor(f"bank{i}", [128, 512], fp32)) for i in range(8)]

        w_in = sem("w_in")
        s_pe, s_act, s_dve, s_pool = sem("s_pe"), sem("s_act"), sem("s_dve"), sem("s_pool")
        loads = [
            (dft[:, :], ins["dft"]), (ident[:, :], ins["ident"]), (mel2[:, :], ins["mel2"]),
            (dctx[:, :], ins["dctx"]), (pd[:, DIM:HW], ins["dctxT"]), (wpb[:, :], ins["wpb"]),
            (wqk_a[:, :, 0:DIM], ins["wq"].rearrange("(t p) n -> p t n", t=2)),
            (wqk_a[:, :, DIM:2 * DIM], ins["wk"].rearrange("(t p) n -> p t n", t=2)),
            (wv_a[:, :, :], ins["wv"].rearrange("(t p) n -> p t n", t=2)),
            (wo_a[:, :, :], ins["wo"].rearrange("(t p) n -> p t n", t=2)),
            (projb[:, :], ins["projb"]),
            (eq_c[:, :], ins["eq"]), (ek_c[:, :], ins["ek"]), (selq[:, :], ins["selq"]),
            (selk[:, :], ins["selk"]), (bd[:, :], ins["bd"]), (blk[:, :], ins["blk"]), (causal[:, :], ins["causal"]),
            (f_wqk[0:KT, :, :], ins["f_wqk"].rearrange("(t p) n -> p t n", t=2)),
            (f_wqk[KT:KT + 1, 1, :], ins["f_bqk"]),
            (f_wv[0:KT, :, :].rearrange("p t (e d) -> p t e d", e=NE)[:, 0, :, :], ins["f_wv"][:, 0:KT, :].rearrange("e p d -> p e d")),
            (f_wv[0:KT, :, :].rearrange("p t (e d) -> p t e d", e=NE)[:, 1, :, :], ins["f_wv"][:, KT:DIM, :].rearrange("e p d -> p e d")),
            (f_wv[KT:KT + 1, 1, :], ins["f_bv"]),
            (f_wp[0:KT, :, :], ins["f_wp"].rearrange("(t p) n -> p t n", t=2)),
            (f_wp[KT:KT + 1, 1, :], ins["f_bp"]),
            (f_wg1[0:KT, :, :], ins["f_wg1"].rearrange("(t p) n -> p t n", t=2)),
            (f_wg1[KT:KT + 1, 1, :], ins["f_bg1"]),
            (f_wg2[0:32, :], ins["f_wg2"]), (f_wg2[32:33, :], ins["f_bg2"]),
            (f_cw[:, :], ins["f_cw"]), (f_cb[:, :], ins["f_cb"]),
        ]
        def rep(x, lo, n):
            return a6[:, x, lo:lo + n]

        chunks = [(w_raw, slice(0, 2 * DIM), KY, selk, None,
                   [(wpcT6[:, t, :], wqk_a[:, t, :]) for t in range(2)])]
        for half in range(2):
            cols = slice(half * HH * M, (half + 1) * HH * M)
            chunks.append((w_q0, cols, KY, selk, None, [(rep(half, KB, KY), projb[:, :])]))
            chunks.append((w_ke, cols, KZ, selk, ek_c, [(rep(2 + half, KB, KZ), projb[:, :])]))
            chunks.append((w_qe, cols, KZ, selq, eq_c, [(rep(half, 0, KZ), projb[:, :])]))

        with nc.Block() as block:
            @block.sync
            def _(sp):
                for n, (dst, src) in enumerate(loads):
                    if n % 2 == 0:
                        sp.dma_start(dst, src).then_inc(w_in, 16)

            @block.scalar
            def _(act):
                for n, (dst, src) in enumerate(loads):
                    if n % 2 == 1:
                        act.dma_start(dst, src).then_inc(w_in, 16)

            @block.gpsimd
            def _(pool):
                nc.gpsimd.memset(yk_all[:, :, :, :], 0.0).then_inc(s_pool, 1)
                pool.wait_ge(s_pool, 1)
                nc.gpsimd.memset(yk_all[:, :, 0, NY:NY + 1], 1.0)
                nc.gpsimd.memset(onesb[:, :], 1.0)
                nc.gpsimd.memset(ones[:, :], 1.0)
                nc.gpsimd.memset(log_eps[:, :], LOG_EPS)
                nc.gpsimd.memset(neg_half[:, :], -0.5)
                nc.gpsimd.memset(a6[:, :, :], 0.0).then_inc(s_pool, 1)

            @block.tensor
            def _(pe):
                pe.wait_ge(w_in, 16 * len(loads))
                nc.tensor.matmul(bank[0][0:NMEL + 1, 0:DIM], dctx[:, :], wpb[:, :], start=True, stop=True)\
                    .then_inc(s_pe, 1)
                pe.wait_ge(s_dve, 1)
                for t in range(2):
                    last = nc.tensor.transpose(bank[1][0:KT, t * NY:(t + 1) * NY],
                                               wpc[:, t * KT:(t + 1) * KT], ident[0:NY, 0:NY])
                last.then_inc(s_pe, 1)
                pe.wait_ge(s_dve, 2)
                for n in range(6):
                    w = wv_a if n >= 4 else wqk_a
                    c = (n % 2 if n >= 4 else n) * KT
                    for t in range(2):
                        last = nc.tensor.matmul(bank[2][0:KT, n * NY:(n + 1) * NY], w[:, t, c:c + KT],
                                                wpcT[:, t, :], start=(t == 0), stop=(t == 1))
                last.then_inc(s_pe, 1)
                pe.wait_ge(s_dve, 3)
                for half in range(2):
                    last = nc.tensor.matmul(bank[3][0:HH * NY, half * DIM:(half + 1) * DIM], avT[:, half, :],
                                            wo_a[:, half, :], start=True, stop=True)
                last.then_inc(s_pe, 1)
                for n, (dst, cols, rows, sel, add, terms) in enumerate(chunks):
                    if n >= 4:
                        pe.wait_ge(s_dve, 4 + n - 4 + 1)
                    for t, (l, r) in enumerate(terms):
                        last = nc.tensor.matmul(bank[4 + n % 4][0:rows, 0:HH * M], l, r, start=(t == 0),
                                                stop=(t == len(terms) - 1))
                    last.then_inc(s_pe, 1)

            @block.vector
            def _(dve):
                chain = sem("setup_chain")
                done = [0]

                def link(i):
                    done[0] += 1
                    i.then_inc(chain, 1)
                    dve.wait_ge(chain, done[0])

                dve.wait_ge(w_in, 16 * len(loads))
                link(nc.vector.tensor_copy(identb[:, :], ident[:, :]))
                for e in range(NE):
                    link(nc.vector.tensor_copy(causalb[:, e, :], causal[:, :]))
                link(nc.vector.reduce_sum(wrow[:, 0:1], wpb[:, :], AX))
                link(nc.vector.tensor_scalar(wrow[:, 1:2], wrow[:, 0:1], 1.0 / DIM, None, ALU.mult))
                link(nc.vector.tensor_scalar(wpc[:, :], wpb[:, :], wrow[:, 1:2], None, ALU.subtract))
                nc.vector.engine_nop().then_inc(s_dve, 1)
                dve.wait_ge(s_pe, 1)
                link(nc.vector.tensor_copy(pd[:, 0:DIM], bank[0][0:NMEL + 1, 0:DIM]))
                dve.wait_ge(s_pe, 2)
                link(nc.vector.tensor_copy(wpcT[:, :, :], bank[1][0:KT, 0:2 * NY].rearrange("p (t n) -> p t n", t=2)))
                for t in range(2):
                    link(nc.vector.tensor_copy(
                        wpcT6[:, t, :].rearrange("p (r n) -> p r n", n=NY),
                        wpcT[:, t:t + 1, :].broadcast_to([KT, len(PAIRS), NY])))
                nc.vector.engine_nop().then_inc(s_dve, 1)
                dve.wait_ge(s_pe, 3)
                dve.wait_ge(s_pool, 2)
                for n in range(4):
                    src = bank[2][0:KT, n * NY:(n + 1) * NY].rearrange("p (r n) -> p r n", r=1)
                    link(nc.vector.tensor_scalar(
                        a6[:, n, KB:KB + KY].rearrange("p (r n) -> p r n", n=NY),
                        src.broadcast_to([KT, len(PAIRS), NY]), 0.5, None, ALU.mult))
                for n in range(2):
                    src = bank[2][0:KT, (4 + n) * NY:(5 + n) * NY].rearrange("p (r n) -> p r n", r=1)
                    link(nc.vector.tensor_tensor(
                        avT[:, n, :].rearrange("p (r n) -> p r n", n=NY),
                        src.broadcast_to([KT, HH, NY]), blk[:, :].rearrange("p (r n) -> p r n", n=NY), ALU.mult))
                nc.vector.engine_nop().then_inc(s_dve, 1)
                dve.wait_ge(s_pe, 4)
                link(nc.vector.tensor_copy(w_vo[:, :, :], bank[3][0:HH * NY, 0:2 * DIM].rearrange("p (t n) -> p t n", t=2)))
                nc.vector.engine_nop().then_inc(s_dve, 1)
                for n, (dst, cols, rows, sel, add, terms) in enumerate(chunks):
                    dve.wait_ge(s_pe, 5 + n)
                    b = bank[4 + n % 4][0:rows, 0:HH * M]
                    p0, p1, p2, r, a = (x[0:rows, :] for x in (*part, rest, acc))
                    link(nc.vector.tensor_copy(p0, b))
                    link(nc.vector.tensor_tensor(r, b, p0, ALU.subtract))
                    nc.vector.engine_nop().then_inc(s_dve, 1)
                    link(nc.vector.tensor_copy(p1, r))
                    link(nc.vector.tensor_tensor(p2, r, p1, ALU.subtract))
                    if add is None:
                        link(nc.vector.tensor_scalar(a, p0, sel[0:rows, 0:1], None, ALU.mult))
                    else:
                        link(nc.vector.scalar_tensor_tensor(a, p0, sel[0:rows, 0:1], add[0:rows, cols],
                                                            ALU.mult, ALU.add))
                    link(nc.vector.scalar_tensor_tensor(a, p1, sel[0:rows, 1:2], a, ALU.mult, ALU.add))
                    link(nc.vector.scalar_tensor_tensor(dst[0:rows, cols], p2, sel[0:rows, 2:3], a, ALU.mult, ALU.add))

        tokens(nc, sem, bank, ins, out, locals())
        attention(nc, sem, bank, ins, out, locals())
        ffn(nc, sem, bank, ins, out, locals())


def pipeline(eng, step, items, unroll, skew, peel=0):
    first = -(-max(skew, peel) // unroll)
    for t in range(first * unroll):
        step(t, t % unroll, t // unroll)
    with eng.Fori(first, items // unroll) as i:
        for j in range(unroll):
            step(i * unroll + j, j, i)
    for t in range(items, items + skew):
        step(t, t % unroll, t // unroll)


def there(t, items):
    return not isinstance(t, int) or 0 <= t < items


def wait(eng, s, n):
    if not isinstance(n, int) or n > 0:
        eng.wait_ge(s, n)


COUNTS = itertools.count()


def wait_apart(eng, s, n, *others):
    if isinstance(n, int):
        for x in (*others, (s, n)):
            wait(eng, *x)
        return
    with eng.register(f"count{next(COUNTS)}") as r:
        eng.reg_add(r, n, 0)
        for x in others:
            wait(eng, *x)
        eng.wait_ge(s, 1)
        eng.wait_ge(s, r)


def with_exitstack_sb(phase):
    def run(nc, sem, *rest):
        with ExitStack() as own:
            phase(nc, lambda name, shape, dt=mybir.dt.float32: own.enter_context(nc.sbuf_tensor(name, shape, dt)),
                  sem, *rest)
    return run


@with_exitstack_sb
def tokens(nc, sb, sem, bank, ins, out, v):
    fp32, bf16 = mybir.dt.float32, mybir.dt.bfloat16
    ALU, ACT = mybir.AluOpType, mybir.ActivationFunctionType
    ident, identb, dft, mel2, pd = v["ident"], v["identb"], v["dft"], v["mel2"], v["pd"]
    h_all, zt_all, ysT_all, y_all, yk_all = v["h_all"], v["zt_all"], v["ysT_all"], v["y_all"], v["yk_all"]
    log_eps, neg_half = v["log_eps"], v["neg_half"]
    T = G * S

    xg = [sb(f"xg{i}", [S, G, FRAME]) for i in range(2)]
    xT = [sb(f"xT{i}", [FRAME, T]) for i in range(2)]
    power = [sb(f"power{i}", [NPOW, T]) for i in range(2)]
    logE = [sb(f"logE{i}", [NMEL + 1, T]) for i in range(2)]
    stats = [sb(f"stats{i}", [S, G, 6]) for i in range(2)]
    mv = [sb(f"mv{i}", [S, G, 2]) for i in range(2)]
    vare = [sb(f"vare{i}", [S, G]) for i in range(2)]
    rstd = [sb(f"rstd{i}", [S, G]) for i in range(2)]
    yrest = sb("yrest", [S, G, NY])

    x_in = [sem(f"x_in{i}") for i in range(2)]
    p_xT, p_dft, p_mel, p_hy, p_ysT = (sem(n) for n in ("p_xT", "p_dft", "p_mel", "p_hy", "p_ysT"))
    a_xT, a_pow, a_log, a_h = (sem(n) for n in ("a_xT", "a_pow", "a_log", "a_h"))
    d_stat, d_y, d_ysT, d_var, d_aggr = (sem(n) for n in ("d_stat", "d_y", "d_ysT", "d_var", "d_aggr"))
    g_rstd, g_yk, g_ones = sem("g_rstd"), sem("g_yk"), sem("g_ones")
    B_XT, B_DFT, B_MEL, B_HY, B_YST = bank[0], bank[1], bank[2], bank[3:5], bank[5]
    SKEW = 6
    frames = ins["x"].rearrange("b (f s) -> f b s", s=STEP)

    def gsl(t):
        return bass.ds(t * G, G)

    with nc.Block() as block:
        @block.sync
        def _(sp):
            def step(t, j, i):
                if there(t, NG):
                    wait(sp, p_xT, t - 1)
                    sp.dma_start(xg[j][:, :, :], frames[:, gsl(t), 0:FRAME]).then_inc(x_in[j], 16)
            pipeline(sp, step, NG, 2, 0, peel=2)

        @block.tensor
        def _(pe):
            def step(t, j, i):
                if there(t, NG):
                    wait(pe, x_in[j], (t - j) * 8 + 16)
                    wait(pe, a_xT, t)
                    for b in range(G):
                        last = nc.tensor.transpose(B_XT[0:FRAME, b * S:(b + 1) * S], xg[j][:, b, :], ident[0:S, 0:S])
                    last.then_inc(p_xT, 1)
                if there(t - 1, NG):
                    wait(pe, a_xT, t)
                    wait(pe, a_pow, t - 1)
                    nc.tensor.matmul(B_DFT[0:NPOW, 0:T], dft[:, :], xT[1 - j][:, :], start=True, stop=True)\
                        .then_inc(p_dft, 1)
                if there(t - 2, NG):
                    wait(pe, a_pow, t - 1)
                    wait(pe, a_log, t - 2)
                    nc.tensor.matmul(B_MEL[0:NMEL, 0:T], mel2[:, :], power[j][:, :], start=True, stop=True)\
                        .then_inc(p_mel, 1)
                if there(t - 3, NG):
                    wait(pe, a_log, t - 2)
                    wait(pe, a_h, t - 3)
                    for b in range(G):
                        last = nc.tensor.matmul(B_HY[b // 2][0:S, (b % 2) * HW:(b % 2 + 1) * HW],
                                                logE[1 - j][:, b * S:(b + 1) * S], pd[:, :], start=True, stop=True)
                    last.then_inc(p_hy, 1)
                if there(t - 5, NG):
                    wait(pe, d_y, 5 * (t - 4))
                    wait(pe, d_ysT, t - 5)
                    for b in range(G):
                        last = nc.tensor.matmul(B_YST[0:KY, b * S:(b + 1) * S], zt_all[:, (t - 5) * G + b, KB:KB + KY],
                                                identb[0:S, 0:S], start=True, stop=True)
                    last.then_inc(p_ysT, 1)
            pipeline(pe, step, NG, 2, SKEW)

        @block.scalar
        def _(act):
            def step(t, j, i):
                if there(t, NG):
                    wait(act, p_xT, t + 1)
                    wait(act, p_dft, t - 1)
                    nc.scalar.activation(xT[j][:, :], B_XT[0:FRAME, 0:T], ACT.Copy).then_inc(a_xT, 1)
                if there(t - 1, NG):
                    wait(act, p_dft, t)
                    wait(act, p_mel, t - 2)
                    nc.scalar.activation(power[1 - j][:, :], B_DFT[0:NPOW, 0:T], ACT.Square).then_inc(a_pow, 1)
                if there(t - 2, NG):
                    if isinstance(t, int) and t == 2:
                        act.wait_ge(g_ones, 2)
                    wait(act, p_mel, t - 1)
                    wait(act, p_hy, t - 4)
                    nc.scalar.activation(logE[j][0:NMEL, :], B_MEL[0:NMEL, 0:T], ACT.Ln, bias=log_eps[0:NMEL, :])\
                        .then_inc(a_log, 1)
                if there(t - 3, NG):
                    wait(act, p_hy, t - 2)
                    for half in range(2):
                        last = nc.scalar.activation(
                            h_all[:, bass.ds((t - 3) * G + 2 * half, 2), :],
                            B_HY[half][0:S, 0:2 * HW].rearrange("p (b n) -> p b n", b=2), ACT.Copy)
                    last.then_inc(a_h, 1)
            pipeline(act, step, NG, 2, SKEW)

        @block.gpsimd
        def _(pool):
            for i in range(2):
                nc.gpsimd.memset(logE[i][:, :], 1.0).then_inc(g_ones, 1)

            def step(t, j, i):
                if there(t - 3, NG):
                    u = 1 - j
                    wait_apart(pool, d_var, t - 2)
                    nc.gpsimd.tensor_tensor(rstd[u][:, :], vare[u][:, :], neg_half[0:S, :], ALU.pow).then_inc(g_rstd, 1)
                if there(t - 5, NG):
                    z = zt_all[:, gsl(t - 5), KB:KB + KY].rearrange("p b (r n) -> p b r n", n=NY)
                    wait_apart(pool, d_y, 5 * (t - 4))
                    nc.gpsimd.tensor_copy(yk_all[:, gsl(t - 5), :, 0:NY], z[:, :, 1::2, :]).then_inc(g_yk, 1)
            pipeline(pool, step, NG, 2, SKEW)

        @block.vector
        def _(dve):
            def step(t, j, i):
                u = 1 - j
                if there(t - 3, NG):
                    wait(dve, a_h, t - 2)
                    for b in range(G):
                        last = nc.vector.bn_stats(stats[u][:, b, :], h_all[:, (t - 3) * G + b, 0:DIM])
                    last.then_inc(d_stat, 1)
                    wait_apart(dve, d_stat, t - 2)
                    for b in range(G):
                        last = nc.vector.bn_aggr(mv[u][:, b, :], stats[u][:, b, :])
                    last.then_inc(d_aggr, 1)
                    wait(dve, d_aggr, t - 2)
                    wait(dve, g_rstd, t - 4)
                    nc.vector.tensor_scalar(vare[u][:, :], mv[u][:, :, 1], LN_EPS, None, ALU.add).then_inc(d_var, 1)
                if there(t - 5, NG):
                    wait(dve, p_ysT, t - 4)
                    nc.vector.tensor_copy(ysT_all[:, gsl(t - 5), :],
                                          B_YST[0:KY, 0:T].rearrange("p (b n) -> p b n", b=G)).then_inc(d_ysT, 1)
                if there(t - 4, NG):
                    c = t - 4
                    y = y_all[:, gsl(c), :]
                    z = zt_all[:, gsl(c), KB:KB + KY].rearrange("p b (r n) -> p b r n", n=NY)
                    wait(dve, g_rstd, c + 1)
                    nc.vector.tensor_tensor(y, h_all[:, gsl(c), DIM:HW],
                                            rstd[j][:, :].rearrange("p (b n) -> p b n", n=1).broadcast_to([S, G, NY]),
                                            ALU.mult).then_inc(d_y, 1)
                    wait(dve, d_y, 5 * c + 1)
                    y4 = y_all[:, gsl(c), :].rearrange("p b (r n) -> p b r n", r=1)
                    nc.vector.tensor_copy(z[:, :, 0:3, :], y4.broadcast_to([S, G, 3, NY])).then_inc(d_y, 1)
                    wait(dve, d_y, 5 * c + 2)
                    nc.vector.tensor_tensor(yrest[:, :, :], y, z[:, :, 0, :], ALU.subtract).then_inc(d_y, 1)
                    wait(dve, d_y, 5 * c + 3)
                    r4 = yrest[:, :, :].rearrange("p b (r n) -> p b r n", r=1)
                    nc.vector.tensor_copy(z[:, :, 3:5, :], r4.broadcast_to([S, G, 2, NY])).then_inc(d_y, 1)
                    wait(dve, d_y, 5 * c + 4)
                    nc.vector.tensor_tensor(z[:, :, 5, :], yrest[:, :, :], z[:, :, 3, :], ALU.subtract).then_inc(d_y, 1)
            pipeline(dve, step, NG, 2, SKEW)


@with_exitstack_sb
def attention(nc, sb, sem, bank, ins, out, v):
    fp32, bf16 = mybir.dt.float32, mybir.dt.bfloat16
    ALU, ACT, AX = mybir.AluOpType, mybir.ActivationFunctionType, mybir.AxisListType.X
    ident, identb, ones = v["ident"], v["identb"], v["ones"]
    w_raw, w_q0, w_qe, w_ke, w_vo = v["w_raw"], v["w_q0"], v["w_qe"], v["w_ke"], v["w_vo"]
    h_all, zt_all, ysT_all, yk_all, onesb, bd = (v[n] for n in ("h_all", "zt_all", "ysT_all", "yk_all", "onesb", "bd"))
    f16 = mybir.dt.float16
    HALF = HH * M
    R1 = NY + 1

    mx_all = sb("mx_all", [S, BATCH, 2 * HEADS])
    dg_all = sb("dg_all", [S, BATCH, 2 * HEADS])
    mxk = sb("mxk", [S, G * HEADS])
    stab = sb("stab", [G * HEADS, 1])
    stabd = sb("stabd", [G * HEADS, G * HEADS])
    off0 = sb("off0", [S, G, 2 * HEADS])
    off = sb("off", [S, G, 2, HEADS])
    orest = sb("orest", [S, G, 2, HEADS])
    sq = [sb(f"sq{i}", [S, 2 * DIM]) for i in range(2)]
    zT = [sb(f"zT{i}", [KZ, 2, S], bf16) for i in range(2)]
    kf = [sb(f"kf{i}", [S, HEADS * M]) for i in range(2)]
    kh = [sb(f"kh{i}", [S, HEADS * M], f16) for i in range(2)]
    kl = [sb(f"kl{i}", [S, HEADS * M], f16) for i in range(2)]
    qf = [sb(f"qf{i}", [128, HH, S]) for i in range(2)]
    qh = [sb(f"qh{i}", [128, HH, 128], f16) for i in range(4)]
    ql = [sb(f"ql{i}", [128, HH, 128], f16) for i in range(4)]
    csum = sb("csum", [128, HH * R1])
    cbd = [sb(f"cbd{i}", [128, HH, 2, R1]) for i in range(2)]
    crest = [sb(f"crest{i}", [128, HH, 2, R1]) for i in range(2)]
    cpart = [[sb(f"cpart{p}{i}", [128, HH, 2, R1], bf16) for p in range(3)] for i in range(4)]
    rden = [sb(f"rden{i}", [S, HEADS]) for i in range(2)]
    rn = [sb(f"rn{i}", [S, HEADS * NY]) for i in range(2)]
    rnT = [sb(f"rnT{i}", [HH * NY, 2, S]) for i in range(2)]

    names = ["raw", "dash", "mxT", "stab", "z", "ek", "eq", "ctx", "num", "numT", "proj"]
    p = {n: sem(f"p_{n}") for n in names}
    a = {n: sem(f"a_{n}") for n in ("sq", "ek", "eq", "z", "c1", "c2", "numT")}
    d = {n: sem(f"d_{n}") for n in ("dg", "max", "mxk", "stab", "off", "csum", "cbd", "crest", "ql", "rden", "num", "h")}
    g = {n: sem(f"g_{n}") for n in ("kl", "ql", "c3", "off", "zero")}
    B_RAW, B_M, B_X, B_T, B_C, B_R = bank[0], bank[1:3], bank[3:5], bank[5], bank[6], bank[7]
    QD = 3
    Z, KQ, CT, NU, TR, PR = 6, 7, 8, 10, 11, 12

    with nc.Block() as block:
        @block.tensor
        def _(pe):
            pe.wait_ge(g["zero"], 8)

            def dash(t, c):
                w = (w_q0, w_ke)[c // 2]
                wait(pe, d["max"], 4 * t + c - 1)
                nc.tensor.matmul(B_M[c % 2][0:S, 0:HALF], ysT_all[:, t, :], w[0:KY, (c % 2) * HALF:(c % 2 + 1) * HALF],
                                 start=True, stop=True).then_inc(p["dash"], 1)

            def step(t, j, i):
                if there(t, BATCH):
                    wait(pe, a["sq"], t)
                    wait(pe, d["h"], t - PR)
                    nc.tensor.matmul(B_RAW[0:S, 0:2 * DIM], ysT_all[:, t, :], w_raw[:, :], start=True, stop=True)\
                        .then_inc(p["raw"], 1)
                    dash(t, 0)
                    dash(t, 1)
                b = t - KQ
                if there(b, BATCH):
                    wait(pe, a["z"], b + 1)
                    for half in range(2):
                        wait(pe, a["eq"], 2 * b - 1 + half)
                        nc.tensor.matmul(B_X[half][0:S, 0:HALF], zT[(j - KQ) % 2][:, 1, :],
                                         w_ke[:, half * HALF:(half + 1) * HALF], start=True, stop=True)\
                            .then_inc(p["ek"], 1)
                b = t - Z
                if there(b, BATCH):
                    wait(pe, g["off"], b - (j - Z) % G + G)
                    wait(pe, a["z"], b)
                    if j == 0 and there(t - 4, BATCH):
                        wait(pe, d["stab"], 2 * i - 1)
                    if j == 1 and there(t - 5, BATCH):
                        wait(pe, d["off"], 3 * i)
                    for n, lo in enumerate((0, KB)):
                        last = nc.tensor.matmul(B_T[0:KZ, n * S:(n + 1) * S], zt_all[:, b, lo:lo + KZ], identb[0:S, 0:S],
                                                start=True, stop=True)
                    last.then_inc(p["z"], 1)
                if there(t, BATCH):
                    dash(t, 2)
                    dash(t, 3)
                b = t - CT
                if there(b, BATCH):
                    wait(pe, g["kl"], b + 1)
                    wait(pe, a["numT"], b - 3)
                    y = yk_all[:, bass.ds(b, 1), :, :].rearrange("p b r n -> p b (r n)")
                    nc.tensor.matmul(B_C[:, 0:HH * 3 * R1], onesb[0:S, :], y.broadcast_to([S, HH, 3 * R1]),
                                     start=True, stop=False, skip_group_check=True)
                    for n in range(HH):
                        for x in (kh, kl):
                            last = nc.tensor.matmul(B_C[:, n * 3 * R1:(n + 1) * 3 * R1],
                                                    x[(j - CT) % 2][:, n * 128:(n + 1) * 128], y[:, 0, :],
                                                    start=False, stop=(x is kl), skip_group_check=True)
                    last.then_inc(p["ctx"], 1)
                b = t - KQ
                if there(b, BATCH):
                    for half in range(2):
                        wait(pe, a["ek"], 2 * b + 1 + half)
                        for n in range(3):
                            f = (3 * half + n) * 128
                            last = nc.tensor.matmul(B_X[half][:, n * S:(n + 1) * S], w_qe[:, f:f + 128],
                                                    zT[(j - KQ) % 2][:, 0, :], start=True, stop=True)
                        last.then_inc(p["eq"], 1)
                b = t - NU
                if there(b, BATCH):
                    wait(pe, d["ql"], b + 1)
                    wait(pe, g["ql"], b + 1)
                    wait(pe, g["c3"], b + 1)
                    wait(pe, d["num"], b)
                    c = cpart[(j - NU) % 4]
                    for r in range(3):
                        nc.tensor.matmul(B_R[:, 0:HH * 2 * R1], onesb[:, :], c[r][:, :, :, :].rearrange("p n w r -> p (n w r)"),
                                         start=(r == 0), stop=False, skip_group_check=True)
                    for n in range(HH):
                        for x in (qh, ql):
                            for r in range(3):
                                last = nc.tensor.matmul(B_R[:, n * 2 * R1:(n + 1) * 2 * R1], x[(j - NU) % 4][:, n, :],
                                                        c[r][:, n, :, :].rearrange("p w r -> p (w r)"), start=False,
                                                        stop=(x is ql and r == 2), skip_group_check=True)
                    last.then_inc(p["num"], 1)
                b = t - TR
                if there(b, BATCH):
                    wait(pe, d["num"], b + 1)
                    if there(t - CT, BATCH):
                        wait(pe, d["csum"], t - CT + 1)
                    else:
                        wait(pe, a["numT"], b)
                    for n in range(2):
                        last = nc.tensor.transpose(B_C[0:HH * NY, n * S:(n + 1) * S],
                                                   rn[(j - TR) % 2][:, n * HH * NY:(n + 1) * HH * NY], ident[0:S, 0:S])
                    last.then_inc(p["numT"], 1)
                b = t - PR
                if there(b, BATCH):
                    wait(pe, a["numT"], b + 1)
                    wait(pe, a["sq"], t + 1 if there(t, BATCH) else BATCH)
                    wait(pe, d["h"], b)
                    for n in range(2):
                        last = nc.tensor.matmul(B_RAW[0:S, 0:DIM], rnT[(j - PR) % 2][:, n, :], w_vo[:, n, :],
                                                start=(n == 0), stop=(n == 1))
                    last.then_inc(p["proj"], 1)
                if j == 3 and there(t, BATCH):
                    if there(t - Z, BATCH):
                        wait(pe, a["z"], t - Z + 1)
                    wait_apart(pe, d["mxk"], i + 1)
                    nc.tensor.transpose(B_T[0:G * HEADS, 0:S], mxk[:, :], ident[0:S, 0:S]).then_inc(p["mxT"], 1)
                if j == 0 and there(t - 4, BATCH):
                    wait(pe, d["stab"], 2 * i)
                    if there(t - Z, BATCH):
                        wait(pe, a["z"], t - Z + 1)
                    nc.tensor.matmul(B_T[0:S, 0:G * HEADS], ones[0:G * HEADS, 0:S], stabd[:, :], start=True, stop=True)\
                        .then_inc(p["stab"], 1)
            pipeline(pe, step, BATCH, 4, PR, peel=PR + 1)

        @block.scalar
        def _(act):
            def step(t, j, i):
                if there(t, BATCH):
                    wait(act, p["raw"], t + 1)
                    wait(act, d["dg"], t - 1)
                    nc.scalar.activation(sq[j % 2][:, :], B_RAW[0:S, 0:2 * DIM], ACT.Square, scale=0.5).then_inc(a["sq"], 1)
                b = t - KQ
                if there(b, BATCH):
                    wait(act, p["ctx"], b - 1)
                    for half in range(2):
                        wait(act, p["ek"], 2 * b + 1 + half)
                        for x in (kf, kh):
                            last = nc.scalar.activation(x[(j - KQ) % 2][:, half * HALF:(half + 1) * HALF],
                                                        B_X[half][0:S, 0:HALF], ACT.Exp)
                        last.then_inc(a["ek"], 1)
                b = t - Z
                if there(b, BATCH):
                    wait(act, p["z"], b + 1)
                    wait(act, p["eq"], 2 * (b - 1))
                    nc.scalar.activation(zT[(j - Z) % 2][:, :, :], B_T[0:KZ, 0:2 * S].rearrange("p (n s) -> p n s", n=2),
                                         ACT.Copy).then_inc(a["z"], 1)
                b = t - KQ
                if there(b, BATCH):
                    wait(act, p["num"], b - 3)
                    wait(act, d["ql"], b - 1)
                    wait(act, g["ql"], b - 1)
                    for half in range(2):
                        wait(act, p["eq"], 2 * b + 1 + half)
                        for x in (qf[(j - KQ) % 2][:, 3 * half:3 * half + 3, :], qh[(j - KQ) % 4][:, 3 * half:3 * half + 3, 0:S]):
                            last = nc.scalar.activation(x, B_X[half][:, 0:3 * S].rearrange("p (n s) -> p n s", n=3), ACT.Exp)
                        last.then_inc(a["eq"], 1)
                for b, n, src, made, done in ((t - CT, 0, cbd, d["cbd"], a["c1"]), (t - CT - 1, 1, crest, d["crest"], a["c2"])):
                    if there(b, BATCH):
                        wait(act, made, b + 1)
                        wait(act, p["num"], b - 3)
                        nc.scalar.activation(cpart[(j - CT - n) % 4][n][:, :, :, :], src[(j - CT - n) % 2][:, :, :, :], ACT.Copy)\
                            .then_inc(done, 1)
                b = t - TR
                if there(b, BATCH):
                    wait(act, p["numT"], b + 1)
                    wait(act, p["proj"], b - 1)
                    nc.scalar.activation(rnT[(j - TR) % 2][:, :, :], B_C[0:HH * NY, 0:2 * S].rearrange("p (n s) -> p n s", n=2),
                                         ACT.Copy).then_inc(a["numT"], 1)
            pipeline(act, step, BATCH, 4, PR, peel=PR + 1)

        @block.vector
        def _(dve):
            def step(t, j, i):
                if j == 0 and there(t - 4, BATCH):
                    wait(dve, p["mxT"], i)
                    nc.vector.reduce_max(stab[:, :], B_T[0:G * HEADS, 0:S], AX).then_inc(d["stab"], 1)
                    wait(dve, d["stab"], 2 * i - 1)
                    nc.vector.tensor_scalar(stabd[:, :], ident[0:G * HEADS, 0:G * HEADS], stab[:, 0:1], None, ALU.mult)\
                        .then_inc(d["stab"], 1)
                if j == 1 and there(t - 5, BATCH):
                    grp = bass.ds(t - 5, G)
                    wait(dve, g["off"], t - 5)
                    nc.vector.tensor_scalar(off0[:, :, :], dg_all[:, grp, :], -0.5, LN_1E4, ALU.mult, ALU.add)\
                        .then_inc(d["off"], 1)
                    wait(dve, d["off"], 3 * i - 2)
                    nc.vector.tensor_tensor(off[:, :, 0, :], off0[:, :, 0:HEADS], mx_all[:, grp, 0:HEADS], ALU.subtract)\
                        .then_inc(d["off"], 1)
                    wait(dve, p["stab"], i)
                    nc.vector.tensor_tensor(off[:, :, 1, :], off0[:, :, HEADS:2 * HEADS],
                                            B_T[0:S, 0:G * HEADS].rearrange("p (b h) -> p b h", b=G), ALU.subtract)\
                        .then_inc(d["off"], 1)
                b = t - CT - 1
                if there(b, BATCH):
                    u = (j - CT - 1) % 2
                    wait(dve, g["c3"], b - 1)
                    wait(dve, a["c1"], b + 1)
                    nc.vector.tensor_tensor(crest[u][:, :, :, :], cbd[u][:, :, :, :], cpart[(j - CT - 1) % 4][0][:, :, :, :],
                                            ALU.subtract).then_inc(d["crest"], 1)
                if there(t, BATCH):
                    for c in range(4):
                        wait(dve, p["dash"], 4 * t + 1 + c)
                        nc.vector.reduce_max(mx_all[:, t, c * HH:(c + 1) * HH],
                                             B_M[c % 2][0:S, 0:HALF].rearrange("p (h m) -> p h m", m=M), AX)\
                            .then_inc(d["max"], 1)
                    wait(dve, a["sq"], t + 1)
                    nc.vector.reduce_sum(dg_all[:, t, :], sq[j % 2][:, :].rearrange("p (h d) -> p h d", d=DH), AX)\
                        .then_inc(d["dg"], 1)
                if j == 3 and there(t, BATCH):
                    wait_apart(dve, d["max"], 4 * t + 4)
                    wait(dve, p["mxT"], i)
                    nc.vector.tensor_copy(mxk[:, :].rearrange("p (b h) -> p b h", b=G),
                                          mx_all[:, bass.ds(t - 3, G), HEADS:2 * HEADS]).then_inc(d["mxk"], 1)
                b = t - CT
                if there(b, BATCH):
                    wait(dve, p["ctx"], b + 1)
                    nc.vector.reduce_sum(csum[:, :].rearrange("p (n r) -> p n r", n=HH),
                                         B_C[:, 0:HH * 3 * R1].rearrange("p (n w r) -> p n r w", n=HH, w=3), AX)\
                        .then_inc(d["csum"], 1)
                    wait(dve, d["csum"], b + 1)
                    wait(dve, a["c1"], b - 1)
                    nc.vector.tensor_tensor(cbd[(j - CT) % 2][:, :, :, :],
                                            csum[:, :].rearrange("p (n w r) -> p n w r", n=HH, w=1).broadcast_to([128, HH, 2, R1]),
                                            bd[:, :].rearrange("p (n w r) -> p n w r", n=1, r=1).broadcast_to([128, HH, 2, R1]),
                                            ALU.mult).then_inc(d["cbd"], 1)
                b = t - NU
                if there(b, BATCH):
                    u = (j - NU) % 2
                    num = B_R[0:S, 0:HEADS * R1].rearrange("p (h r) -> p h r", h=HEADS)
                    wait(dve, p["num"], b + 1)
                    nc.vector.reciprocal(rden[u][:, :], num[:, :, NY]).then_inc(d["rden"], 1)
                    wait(dve, d["rden"], b + 1)
                    wait(dve, p["numT"], b - 1)
                    nc.vector.tensor_tensor(rn[u][:, :].rearrange("p (h r) -> p h r", h=HEADS), num[:, :, 0:NY],
                                            rden[u][:, :].rearrange("p (h r) -> p h r", r=1).broadcast_to([S, HEADS, NY]),
                                            ALU.mult).then_inc(d["num"], 1)
                b = t - KQ
                if there(b, BATCH):
                    wait(dve, a["eq"], 2 * b + 2)
                    wait(dve, p["num"], b - 3)
                    nc.vector.tensor_tensor(ql[(j - KQ) % 4][:, 0:QD, 0:S], qf[(j - KQ) % 2][:, 0:QD, :],
                                            qh[(j - KQ) % 4][:, 0:QD, 0:S], ALU.subtract).then_inc(d["ql"], 1)
                b = t - PR
                if there(b, BATCH):
                    wait(dve, p["proj"], b + 1)
                    nc.vector.tensor_tensor(h_all[:, b, 0:DIM], B_RAW[0:S, 0:DIM], h_all[:, b, 0:DIM], ALU.add)\
                        .then_inc(d["h"], 1)
            pipeline(dve, step, BATCH, 4, PR, peel=PR + 1)

        @block.gpsimd
        def _(pool):
            for i in range(4):
                nc.gpsimd.memset(qh[i][:, :, S:128], 0.0).then_inc(g["zero"], 1)
                nc.gpsimd.memset(ql[i][:, :, S:128], 0.0).then_inc(g["zero"], 1)

            def step(t, j, i):
                b = t - CT - 2
                if there(b, BATCH):
                    wait_apart(pool, a["c2"], b + 1, (p["num"], b - 3))
                    nc.gpsimd.tensor_tensor(cpart[(j - CT - 2) % 4][2][:, :, :, :], crest[(j - CT) % 2][:, :, :, :],
                                            cpart[(j - CT - 2) % 4][1][:, :, :, :], ALU.subtract).then_inc(g["c3"], 1)
                if j == 1 and there(t - 5, BATCH):
                    c = t - 5
                    z = zt_all[:, bass.ds(c, G), :].rearrange("p b (w c) -> p b w c", w=2)
                    wait_apart(pool, d["off"], 3 * i)
                    nc.gpsimd.tensor_copy(z[:, :, :, 0:HEADS], off[:, :, :, :]).then_inc(g["off"], 1)
                    wait_apart(pool, g["off"], c + 1)
                    nc.gpsimd.tensor_tensor(orest[:, :, :, :], off[:, :, :, :], z[:, :, :, 0:HEADS], ALU.subtract)\
                        .then_inc(g["off"], 1)
                    wait_apart(pool, g["off"], c + 2)
                    nc.gpsimd.tensor_copy(z[:, :, :, HEADS:2 * HEADS], orest[:, :, :, :]).then_inc(g["off"], 1)
                    wait_apart(pool, g["off"], c + 3)
                    nc.gpsimd.tensor_tensor(z[:, :, :, 2 * HEADS:3 * HEADS], orest[:, :, :, :],
                                            z[:, :, :, HEADS:2 * HEADS], ALU.subtract).then_inc(g["off"], 1)
                b = t - KQ
                if there(b, BATCH):
                    wait_apart(pool, a["ek"], 2 * b + 2, (p["ctx"], b - 1))
                    nc.gpsimd.tensor_tensor(kl[(j - KQ) % 2][:, :], kf[(j - KQ) % 2][:, :], kh[(j - KQ) % 2][:, :],
                                            ALU.subtract).then_inc(g["kl"], 1)
                if there(b, BATCH):
                    wait_apart(pool, a["eq"], 2 * b + 2, (p["num"], b - 3))
                    nc.gpsimd.tensor_tensor(ql[(j - KQ) % 4][:, QD:HH, 0:S], qf[(j - KQ) % 2][:, QD:HH, :],
                                            qh[(j - KQ) % 4][:, QD:HH, 0:S], ALU.subtract).then_inc(g["ql"], 1)
            pipeline(pool, step, BATCH, 4, PR, peel=PR + 1)


@with_exitstack_sb
def ffn(nc, sb, sem, bank, ins, out, v):
    fp32, bf16 = mybir.dt.float32, mybir.dt.bfloat16
    ALU, ACT, AX = mybir.AluOpType, mybir.ActivationFunctionType, mybir.AxisListType.X
    ident, identb, causalb, neg_half = v["ident"], v["identb"], v["causalb"], v["neg_half"]
    f_wqk, f_wv, f_wp, f_wg1, f_wg2, f_cw, f_cb = (v[n] for n in ("f_wqk", "f_wv", "f_wp", "f_wg1", "f_wg2", "f_cw", "f_cb"))
    h_all = v["h_all"]
    T, V1, NH = G * S, HD + 1, 32
    SCALE = HD ** -0.5

    stats = [sb(f"f_stats{i}", [S, 6]) for i in range(2)]
    mv = [sb(f"f_mv{i}", [S, 2]) for i in range(2)]
    vare = [sb(f"f_vare{i}", [S, 1]) for i in range(2)]
    rstd = [sb(f"f_rstd{i}", [S, 1]) for i in range(2)]
    z = [sb(f"f_z{i}", [S, DIM]) for i in range(2)]
    zT = [sb(f"f_zT{i}", [KT + 1, 2, G, S]) for i in range(2)]
    hid = [sb(f"f_hid{i}", [NH + 1, G, S]) for i in range(2)]
    q0 = [sb(f"f_q0{i}", [HD, G, S + 2]) for i in range(2)]
    q0c = [sb(f"f_q0c{i}", [128, G, S]) for i in range(2)]
    q1 = [sb(f"f_q1{i}", [128, G, S]) for i in range(2)]
    k01 = [sb(f"f_k01{i}", [128, G, S]) for i in range(2)]
    qk2 = [sb(f"f_qk2{i}", [128, G, S]) for i in range(2)]
    k2 = [sb(f"f_k2{i}", [128, G, S]) for i in range(2)]
    vv = [sb(f"f_v{i}", [S, NE, V1]) for i in range(8)]
    smax = [sb(f"f_smax{i}", [S, NE]) for i in range(2)]
    prob = [sb(f"f_prob{i}", [S, NE, S]) for i in range(2)]
    probT = [sb(f"f_probT{i}", [S, NE, S]) for i in range(2)]
    rden = [sb(f"f_rden{i}", [S, NE]) for i in range(2)]
    mixw = [sb(f"f_mixw{i}", [S, NE]) for i in range(2)]
    mixed = [sb(f"f_mixed{i}", [S, DIM]) for i in range(2)]
    mixT = [sb(f"f_mixT{i}", [KT + 1, 2, S]) for i in range(2)]
    lmax, lexp, lsum, lrec = sb("f_lmax", [S, G]), sb("f_lexp", [S, G, NE]), sb("f_lsum", [S, G]), sb("f_lrec", [S, G])
    gate, gexp = sb("f_gate", [S, G, NE]), sb("f_gexp", [S, G, NE])
    less, both, keep = sb("f_less", [S, G, 3]), sb("f_both", [S, G]), sb("f_keep", [S, G, NE])
    drop = sb("f_drop", [S, G, 2])
    gsum, grec = sb("f_gsum", [S, G]), sb("f_grec", [S, G])
    top = [sb(f"f_top{i}", [S, G, NE]) for i in range(2)]

    p = {n: sem(f"fp_{n}") for n in ("zT", "tile", "v", "logit", "score", "probT", "mix", "mixT", "out")}
    a = {n: sem(f"fa_{n}") for n in ("zT", "tile", "v", "lexp", "prob", "gexp", "probT", "mixT")}
    d = {n: sem(f"fd_{n}") for n in ("stat", "aggr", "var", "z", "conv", "smax", "prob", "lmax", "lsub", "lsum", "lrec",
                                     "gsum", "grec", "top", "rden", "mixw", "mix", "out")}
    g = {n: sem(f"fg_{n}") for n in ("set", "rstd", "gate", "shift", "less", "keep", "kept")}
    stored = sem("stored")
    B_ZT, B_TILE, B_V, B_S, B_PT, B_MIX, B_OUT = bank[0], bank[1:3], bank[3], bank[4], bank[5], bank[6], bank[7]
    ZS, ZT, TL, VS, LG, CV, SC, PT, MX, MT, OT = 1, 2, 6, 7, 7, 8, 11, 12, 13, 14, 15
    N_SET = 24

    def col(x):
        return x.rearrange("p (b n) -> p b n", n=1)

    with nc.Block() as block:
        @block.sync
        def _(sp):
            def step(t, j, i):
                b = t - OT
                if there(b, BATCH):
                    wait(sp, d["out"], b + 1)
                    sp.dma_start(out[b, :, :], h_all[:, b, 0:DIM]).then_inc(stored, 16)
            pipeline(sp, step, BATCH, 8, OT)
            sp.wait_ge(stored, 16 * BATCH)

        @block.tensor
        def _(pe):
            pe.wait_ge(g["set"], N_SET)

            def step(t, j, i):
                b = t - OT
                if there(b, BATCH):
                    wait(pe, a["mixT"], b + 1)
                    for n in range(2):
                        last = nc.tensor.matmul(B_OUT[0:S, 0:DIM], mixT[(j - OT) % 2][0:KT + n, n, :], f_wp[0:KT + n, n, :],
                                                start=(n == 0), stop=(n == 1))
                    last.then_inc(p["out"], 1)
                b = t - ZT
                if there(b, BATCH):
                    wait(pe, d["z"], b + 1)
                    wait(pe, a["zT"], b)
                    if (j - LG - 1) % 4 == 0 and there(t - LG - 1, BATCH):
                        wait(pe, d["lsub"], groups(i, j, LG + 1) + 1)
                    for n in range(2):
                        last = nc.tensor.transpose(B_ZT[0:KT, n * S:(n + 1) * S], z[(j - ZT) % 2][:, n * KT:(n + 1) * KT],
                                                   ident[0:S, 0:S])
                    last.then_inc(p["zT"], 1)
                b = t - SC
                if there(b, BATCH):
                    u, s = (j - SC) % 8 // 4, (j - SC) % 4
                    wait(pe, a["tile"], b - s + 4)
                    wait(pe, d["conv"], 3 * groups(i, j, SC) + 3)
                    wait(pe, d["prob"], b)
                    nc.tensor.matmul(B_S[0:S, 0:NE * S], identb[0:S, 0:S], causalb[:, :, :].rearrange("p e s -> p (e s)"),
                                     start=True, stop=False, skip_group_check=True)
                    for e, (ql, kr) in enumerate([(q0c[u], k01[u]), (q1[u], k01[u]), (qk2[u], k2[u])]):
                        last = nc.tensor.matmul(B_S[0:S, e * S:(e + 1) * S], ql[:, s, :], kr[:, s, :], start=False, stop=(e == NE - 1),
                                                skip_group_check=True)
                    last.then_inc(p["score"], 1)
                b = t - TL
                if there(b, BATCH):
                    u, n = (j - TL) % 8 // 4, (j - TL) % 4
                    wait(pe, a["zT"], b - n + 4)
                    wait(pe, a["tile"], b - 1)
                    rows = NH if n == 0 else 128
                    for k in range(2):
                        w = f_wg1[0:KT + k, k, :] if n == 0 else f_wqk[0:KT + k, k, (n - 1) * 128:n * 128]
                        last = nc.tensor.matmul(B_TILE[n % 2][0:rows, 0:T], w, zT[u][0:KT + k, k, :, :].rearrange("p b s -> p (b s)"),
                                                start=(k == 0), stop=(k == 1))
                    last.then_inc(p["tile"], 1)
                b = t - VS
                if there(b, BATCH):
                    u, s = (j - VS) % 8 // 4, (j - VS) % 4
                    wait(pe, a["v"], b)
                    for k in range(2):
                        last = nc.tensor.matmul(B_V[0:S, 0:DIM], zT[u][0:KT + k, k, s, :], f_wv[0:KT + k, k, :],
                                                start=(k == 0), stop=(k == 1))
                    last.then_inc(p["v"], 1)
                b = t - PT
                if there(b, BATCH):
                    wait(pe, a["prob"], b + 1)
                    wait(pe, a["probT"], b)
                    for e in range(NE):
                        last = nc.tensor.transpose(B_PT[0:S, e * S:(e + 1) * S], prob[(j - PT) % 2][:, e, :], ident[0:S, 0:S])
                    last.then_inc(p["probT"], 1)
                b = t - LG
                if (j - LG) % 4 == 0 and there(b, BATCH):
                    u = (j - LG) % 8 // 4
                    wait(pe, a["tile"], b + 1)
                    wait(pe, a["zT"], t - ZT + 1 if there(t - ZT, BATCH) else BATCH)
                    for s in range(G):
                        last = nc.tensor.matmul(B_ZT[0:S, s * NE:(s + 1) * NE], hid[u][:, s, :], f_wg2[:, :], start=True, stop=True)
                    last.then_inc(p["logit"], 1)
                b = t - MX
                if there(b, BATCH):
                    wait(pe, a["probT"], b + 1)
                    wait(pe, a["v"], b + 1)
                    wait(pe, d["mix"], b)
                    for e in range(NE):
                        last = nc.tensor.matmul(B_MIX[0:S, e * V1:(e + 1) * V1], probT[(j - MX) % 2][:, e, :],
                                                vv[(j - MX) % 8][:, e, :], start=True, stop=True)
                    last.then_inc(p["mix"], 1)
                b = t - MT
                if there(b, BATCH):
                    wait(pe, d["mix"], b + 1)
                    wait(pe, d["out"], b)
                    for n in range(2):
                        last = nc.tensor.transpose(B_OUT[0:KT, n * S:(n + 1) * S], mixed[(j - MT) % 2][:, n * KT:(n + 1) * KT],
                                                   ident[0:S, 0:S])
                    last.then_inc(p["mixT"], 1)
            pipeline(pe, step, BATCH, 8, OT)

        @block.scalar
        def _(act):
            act.wait_ge(g["set"], N_SET)

            def step(t, j, i):
                b = t - ZT
                if there(b, BATCH):
                    u, s = (j - ZT) % 8 // 4, (j - ZT) % 4
                    wait(act, p["zT"], b + 1)
                    wait(act, p["v"], b - 7)
                    wait(act, p["tile"], b - s - 4)
                    nc.scalar.activation(zT[u][0:KT, :, s, :], B_ZT[0:KT, 0:2 * S].rearrange("p (n s) -> p n s", n=2),
                                         ACT.Copy).then_inc(a["zT"], 1)
                b = t - TL
                if there(b, BATCH):
                    u, n = (j - TL) % 8 // 4, (j - TL) % 4
                    wait(act, p["tile"], b + 1)
                    src = B_TILE[n % 2][:, 0:T].rearrange("p (b s) -> p b s", b=G)
                    if n == 0:
                        wait(act, p["logit"], groups(i, j, TL) - 1)
                        nc.scalar.activation(hid[u][0:NH, :, :], src[0:NH, :, :], ACT.Relu).then_inc(a["tile"], 1)
                    elif n == 1:
                        wait(act, p["score"], b - n - 4)
                        nc.scalar.activation(q1[u][HD:128, :, :], src[HD:128, :, :], ACT.Copy)
                        nc.scalar.activation(q0[u][:, :, 1:S + 1], src[0:HD, :, :], ACT.Copy).then_inc(a["tile"], 1)
                    elif n == 2:
                        nc.scalar.activation(k01[u][:, :, :], src, ACT.Copy).then_inc(a["tile"], 1)
                    else:
                        nc.scalar.activation(qk2[u][:, :, :], src, ACT.Copy)
                        nc.scalar.activation(k2[u][0:HD, :, :], src[HD:128, :, :], ACT.Copy).then_inc(a["tile"], 1)
                b = t - VS
                if there(b, BATCH):
                    wait(act, p["v"], b + 1)
                    wait(act, p["mix"], b - 7)
                    nc.scalar.activation(vv[(j - VS) % 8][:, :, 0:HD], B_V[0:S, 0:DIM].rearrange("p (e d) -> p e d", e=NE),
                                         ACT.Copy).then_inc(a["v"], 1)
                b = t - SC
                if there(b, BATCH):
                    wait(act, d["prob"], b + 1)
                    x = prob[(j - SC) % 2]
                    nc.scalar.activation(x[:, :, :], x[:, :, :], ACT.Exp, scale=SCALE).then_inc(a["prob"], 1)
                b = t - PT
                if there(b, BATCH):
                    wait(act, p["probT"], b + 1)
                    wait(act, p["mix"], b - 1)
                    nc.scalar.activation(probT[(j - PT) % 2][:, :, :], B_PT[0:S, 0:NE * S].rearrange("p (e s) -> p e s", e=NE),
                                         ACT.Copy).then_inc(a["probT"], 1)
                b = t - LG
                if (j - LG) % 4 == 0 and there(b, BATCH):
                    wait(act, d["lsub"], groups(i, j, LG) + 1)
                    nc.scalar.activation(lexp[:, :, :], lexp[:, :, :], ACT.Exp).then_inc(a["lexp"], 1)
                b = t - LG - 2
                if (j - LG - 2) % 4 == 0 and there(b, BATCH):
                    wait(act, g["shift"], groups(i, j, LG + 2) + 1)
                    nc.scalar.activation(gexp[:, :, :], gexp[:, :, :], ACT.Exp).then_inc(a["gexp"], 1)
                b = t - MT
                if there(b, BATCH):
                    wait(act, p["mixT"], b + 1)
                    wait(act, p["out"], b - 1)
                    nc.scalar.activation(mixT[(j - MT) % 2][0:KT, :, :], B_OUT[0:KT, 0:2 * S].rearrange("p (n s) -> p n s", n=2),
                                         ACT.Copy).then_inc(a["mixT"], 1)
            pipeline(act, step, BATCH, 8, OT)

        @block.vector
        def _(dve):
            dve.wait_ge(g["set"], N_SET)

            def step(t, j, i):
                b = t - OT
                if there(b, BATCH):
                    wait(dve, p["out"], b + 1)
                    nc.vector.tensor_tensor(h_all[:, b, 0:DIM], B_OUT[0:S, 0:DIM], h_all[:, b, 0:DIM], ALU.add)\
                        .then_inc(d["out"], 1)
                b = t
                if there(b, BATCH):
                    u = j % 2
                    nc.vector.bn_stats(stats[u][:, :], h_all[:, b, 0:DIM]).then_inc(d["stat"], 1)
                    wait_apart(dve, d["stat"], b + 1)
                    nc.vector.bn_aggr(mv[u][:, :], stats[u][:, :]).then_inc(d["aggr"], 1)
                    wait(dve, g["rstd"], b - 1)
                    wait(dve, d["aggr"], b + 1)
                    nc.vector.tensor_scalar(vare[u][:, :], mv[u][:, 1:2], LN_EPS, None, ALU.add).then_inc(d["var"], 1)
                b = t - ZS
                if there(b, BATCH):
                    u = (j - ZS) % 2
                    wait(dve, g["rstd"], b + 1)
                    wait(dve, p["zT"], b - 1)
                    nc.vector.tensor_scalar(z[u][:, :], h_all[:, b, 0:DIM], mv[u][:, 0:1], rstd[u][:, 0:1],
                                            ALU.subtract, ALU.mult).then_inc(d["z"], 1)
                b = t - SC
                if there(b, BATCH):
                    u = (j - SC) % 2
                    src = B_S[0:S, 0:NE * S].rearrange("p (e s) -> p e s", e=NE)
                    wait(dve, p["score"], b + 1)
                    nc.vector.reduce_max(smax[u][:, :], src, AX).then_inc(d["smax"], 1)
                    wait(dve, p["probT"], b - 1)
                    wait(dve, d["smax"], b + 1)
                    nc.vector.tensor_tensor(prob[u][:, :, :], src,
                                            smax[u][:, :].rearrange("p (e n) -> p e n", n=1).broadcast_to([S, NE, S]),
                                            ALU.subtract).then_inc(d["prob"], 1)
                b = t - CV
                if (j - CV) % 4 == 0 and there(b, BATCH):
                    u, c = (j - CV) % 8 // 4, groups(i, j, CV)
                    x, y = q0[u][:, :, :], q0c[u][0:HD, :, :]
                    wait(dve, a["tile"], b + 2)
                    wait(dve, p["score"], b - 4)
                    nc.vector.tensor_scalar(y, x[:, :, 1:S + 1], f_cw[:, 1:2], f_cb[:, 0:1], ALU.mult, ALU.add)\
                        .then_inc(d["conv"], 1)
                    wait(dve, d["conv"], 3 * c + 1)
                    nc.vector.scalar_tensor_tensor(y, x[:, :, 0:S], f_cw[:, 0:1], y,
                                                   ALU.mult, ALU.add).then_inc(d["conv"], 1)
                    wait(dve, d["conv"], 3 * c + 2)
                    nc.vector.scalar_tensor_tensor(y, x[:, :, 2:S + 2], f_cw[:, 2:3], y,
                                                   ALU.mult, ALU.add).then_inc(d["conv"], 1)
                b = t - LG
                if (j - LG) % 4 == 0 and there(b, BATCH):
                    c = groups(i, j, LG)
                    lg = B_ZT[0:S, 0:G * NE].rearrange("p (b e) -> p b e", b=G)
                    wait(dve, p["logit"], c + 1)
                    nc.vector.reduce_max(lmax[:, :], lg, AX).then_inc(d["lmax"], 1)
                    wait(dve, d["lmax"], c + 1)
                    wait(dve, g["gate"], c)
                    nc.vector.tensor_tensor(lexp[:, :, :], lg, col(lmax[:, :]).broadcast_to([S, G, NE]), ALU.subtract)\
                        .then_inc(d["lsub"], 1)
                b = t - LG - 1
                if (j - LG - 1) % 4 == 0 and there(b, BATCH):
                    c = groups(i, j, LG + 1)
                    wait(dve, a["lexp"], c + 1)
                    nc.vector.reduce_sum(lsum[:, :], lexp[:, :, :], AX).then_inc(d["lsum"], 1)
                    wait(dve, d["lsum"], c + 1)
                    wait(dve, g["shift"], c)
                    nc.vector.reciprocal(lrec[:, :], lsum[:, :]).then_inc(d["lrec"], 1)
                b = t - LG - 3
                if (j - LG - 3) % 4 == 0 and there(b, BATCH):
                    c, u = groups(i, j, LG + 3), (j - LG - 3) % 8 // 4
                    wait(dve, g["kept"], c + 1)
                    nc.vector.reduce_sum(gsum[:, :], keep[:, :, :], AX).then_inc(d["gsum"], 1)
                    wait(dve, d["gsum"], c + 1)
                    nc.vector.reciprocal(grec[:, :], gsum[:, :]).then_inc(d["grec"], 1)
                    wait(dve, d["grec"], c + 1)
                    nc.vector.tensor_tensor(top[u][:, :, :], keep[:, :, :], col(grec[:, :]).broadcast_to([S, G, NE]), ALU.mult)\
                        .then_inc(d["top"], 1)
                b = t - MX
                if there(b, BATCH):
                    u, w, s = (j - MX) % 2, (j - MX) % 8 // 4, (j - MX) % 4
                    src = B_MIX[0:S, 0:NE * V1].rearrange("p (e d) -> p e d", e=NE)
                    wait(dve, p["mix"], b + 1)
                    nc.vector.reciprocal(rden[u][:, :], src[:, :, HD]).then_inc(d["rden"], 1)
                    wait(dve, d["rden"], b + 1)
                    wait(dve, d["top"], groups(i, j, MX) + 1)
                    nc.vector.tensor_tensor(mixw[u][:, :], rden[u][:, :], top[w][:, s, :], ALU.mult).then_inc(d["mixw"], 1)
                    wait(dve, p["mixT"], b - 1)
                    wait(dve, d["mixw"], b + 1)
                    nc.vector.tensor_tensor(mixed[u][:, :].rearrange("p (e d) -> p e d", e=NE), src[:, :, 0:HD],
                                            mixw[u][:, :].rearrange("p (e n) -> p e n", n=1).broadcast_to([S, NE, HD]),
                                            ALU.mult).then_inc(d["mix"], 1)
            pipeline(dve, step, BATCH, 8, OT)

        @block.gpsimd
        def _(pool):
            for i in range(8):
                nc.gpsimd.memset(vv[i][:, :, HD:V1], 1.0).then_inc(g["set"], 1)
            for i in range(2):
                nc.gpsimd.memset(q0[i][:, :, 0:1], 0.0).then_inc(g["set"], 1)
                nc.gpsimd.memset(q0[i][:, :, S + 1:S + 2], 0.0).then_inc(g["set"], 1)
                nc.gpsimd.memset(q0c[i][:, :, :], 0.0).then_inc(g["set"], 1)
                nc.gpsimd.memset(q1[i][:, :, :], 0.0).then_inc(g["set"], 1)
                nc.gpsimd.memset(k2[i][:, :, :], 0.0).then_inc(g["set"], 1)
            pool.wait_ge(g["set"], 18)
            for i in range(2):
                nc.gpsimd.memset(zT[i][KT:KT + 1, :, :, :], 1.0).then_inc(g["set"], 1)
                nc.gpsimd.memset(mixT[i][KT:KT + 1, :, :], 1.0).then_inc(g["set"], 1)
            pool.wait_ge(g["set"], 22)
            for i in range(2):
                nc.gpsimd.memset(hid[i][NH:NH + 1, :, :], 1.0).then_inc(g["set"], 1)
            pool.wait_ge(g["set"], N_SET)

            def step(t, j, i):
                b = t
                if there(b, BATCH):
                    u = j % 2
                    wait(pool, d["z"], b - 1)
                    wait_apart(pool, d["var"], b + 1)
                    nc.gpsimd.tensor_tensor(rstd[u][:, :], vare[u][:, :], neg_half[0:S, 0:1], ALU.pow).then_inc(g["rstd"], 1)
                b = t - LG - 1
                if (j - LG - 1) % 4 == 0 and there(b, BATCH):
                    c = groups(i, j, LG + 1)
                    wait_apart(pool, d["lrec"], c + 1)
                    nc.gpsimd.tensor_tensor(gate[:, :, :], lexp[:, :, :], col(lrec[:, :]).broadcast_to([S, G, NE]), ALU.mult)\
                        .then_inc(g["gate"], 1)
                    wait_apart(pool, g["gate"], c + 1)
                    nc.gpsimd.tensor_tensor(gexp[:, :, :], gate[:, :, :], col(lrec[:, :]).broadcast_to([S, G, NE]), ALU.subtract)\
                        .then_inc(g["shift"], 1)
                    nc.gpsimd.tensor_tensor(less[:, :, 0:2], gate[:, :, 0:1].broadcast_to([S, G, 2]), gate[:, :, 1:3],
                                            ALU.subtract).then_inc(g["less"], 1)
                    nc.gpsimd.tensor_tensor(less[:, :, 2], gate[:, :, 1], gate[:, :, 2], ALU.subtract).then_inc(g["less"], 1)
                    wait_apart(pool, g["less"], 6 * c + 2)
                    nc.gpsimd.tensor_scalar(less[:, :, :], less[:, :, :], 0.0, None, ALU.is_lt).then_inc(g["less"], 1)
                    wait_apart(pool, g["less"], 6 * c + 3)
                    nc.gpsimd.tensor_tensor(drop[:, :, 0], less[:, :, 0], less[:, :, 1], ALU.mult).then_inc(g["less"], 1)
                    nc.gpsimd.tensor_tensor(both[:, :], less[:, :, 0], less[:, :, 2], ALU.mult).then_inc(g["less"], 1)
                    wait_apart(pool, g["less"], 6 * c + 5)
                    nc.gpsimd.tensor_tensor(drop[:, :, 1], less[:, :, 2], both[:, :], ALU.subtract).then_inc(g["less"], 1)
                b = t - LG - 2
                if (j - LG - 2) % 4 == 0 and there(b, BATCH):
                    c = groups(i, j, LG + 2)
                    wait_apart(pool, g["less"], 6 * c + 6)
                    wait_apart(pool, d["top"], c)
                    nc.gpsimd.tensor_scalar(keep[:, :, 0:2], drop[:, :, :], -1.0, 1.0, ALU.mult, ALU.add).then_inc(g["keep"], 1)
                    nc.gpsimd.tensor_tensor(keep[:, :, 2], drop[:, :, 0], drop[:, :, 1], ALU.add).then_inc(g["keep"], 1)
                    wait(pool, a["gexp"], c + 1)
                    wait_apart(pool, g["keep"], 2 * c + 2)
                    nc.gpsimd.tensor_tensor(keep[:, :, :], keep[:, :, :], gexp[:, :, :], ALU.mult).then_inc(g["kept"], 1)
            pipeline(pool, step, BATCH, 8, OT)


def groups(i, j, skew):
    return 2 * i + (j - skew) // 4


def kernel(**inputs):
    import numpy as np
    import concourse.bacc as _bacc
    from concourse.bass_utils import run_bass_kernel_spmd as _run

    x = {k: np.asarray(a) for k, a in inputs.items()}
    f32 = np.float32
    pre = lambda n: x["L0_" + n]
    n, k = np.arange(FRAME), np.arange(NFFT)
    window = 0.54 - 0.46 * np.cos(2.0 * np.pi * n / (FRAME - 1))
    angle = 2.0 * np.pi * np.outer(n, k) / FRAME
    dft = np.concatenate([window[:, None] * np.cos(angle), window[:, None] * np.sin(angle[:, 1:NFFT - 1])], 1)
    one = (np.arange(HEADS)[:, None] == np.arange(HEADS * M)[None, :] // M)
    eq, ek = np.zeros((KZ, HEADS * M), f32), np.zeros((KZ, HEADS * M), f32)
    selq, selk = np.zeros((KZ, 3), f32), np.zeros((KZ, 3), f32)
    for i in range(3):
        eq[i * HEADS:(i + 1) * HEADS] = one
        ek[KY + i * HEADS:KY + (i + 1) * HEADS] = one
    for i, (_, w) in enumerate(PAIRS):
        selq[KB + i * NY:KB + (i + 1) * NY, w] = 1.0
        selk[i * NY:(i + 1) * NY, w] = 1.0
    consts = {
        "dft": dft.astype(f32), "ident": np.eye(128, dtype=f32), "eq": eq, "ek": ek, "selq": selq, "selk": selk,
        "blk": (np.arange(KT)[:, None] // DH == np.arange(HH * NY)[None, :] // NY).astype(f32),
        "bd": (np.arange(128)[:, None] // M == np.arange(2)[None, :]).astype(f32),
        "causal": np.where(np.arange(S)[None, :] > np.arange(S)[:, None], NEG, 0.0).astype(f32),
    }
    mel, dct = pre("tok_mel_filters"), pre("tok_dct")
    dctx = np.zeros((NY, NMEL + 1), f32)
    dctx[0:NMFCC, 0:NMEL] = dct
    dctx[NMFCC, NMEL] = 1.0
    projb = np.zeros((KT, HH * M), f32)
    for h in range(HH):
        projb[h * DH:(h + 1) * DH, h * M:(h + 1) * M] = pre("attn_proj").T
    w = pre("ffn_Wqk")
    order = [0, 1, 3, 4, 2, 5]
    mix = lambda a: np.concatenate([a[..., i * HD:(i + 1) * HD] for i in order], -1)
    arrays = {
        **consts,
        "x": x["x"], "mel2": np.concatenate([mel.T, mel.T[1:NFFT - 1]]), "dctx": dctx, "dctxT": dctx.T,
        "wpb": np.concatenate([pre("tok_w_proj"), pre("tok_b_proj")[None]]),
        "wq": pre("attn_Wq"), "wk": pre("attn_Wk"), "wv": pre("attn_Wv"), "wo": pre("attn_Wo"), "projb": projb,
        "f_wqk": mix(w), "f_bqk": mix(pre("ffn_bqk"))[None], "f_wv": pre("ffn_Wv"), "f_bv": pre("ffn_bv").reshape(1, DIM),
        "f_wp": pre("ffn_Wp"), "f_bp": pre("ffn_bp")[None], "f_wg1": pre("ffn_Wg1"), "f_bg1": pre("ffn_bg1")[None],
        "f_wg2": pre("ffn_Wg2"), "f_bg2": pre("ffn_bg2")[None],
        "f_cw": pre("ffn_conv_w").reshape(HD, 3), "f_cb": pre("ffn_conv_b")[:, None],
    }
    nc = _bacc.Bacc("TRN2", target_bir_lowering=False, num_devices=1)
    feed, ins = {}, {}
    for name, a in arrays.items():
        a = np.ascontiguousarray(a)
        feed[f"in_{name}"] = a
        ins[name] = nc.dram_tensor(f"in_{name}", a.shape, mybir.dt.from_np(a.dtype), kind="ExternalInput").ap()
    out = nc.dram_tensor("out_0", (BATCH, S, DIM), mybir.dt.float32, kind="ExternalOutput").ap()
    audio_tower(nc, ins, out)
    r = _run(nc, [feed], core_ids=[0])
    return r.results[0]["out_0"]
```

```python
import itertools

import concourse.bass as bass
from concourse import mybir
from contextlib import ExitStack, contextmanager

BATCH, AUDIO = 64, 20000
FRAME, STEP = 100, 160
S = 1 + (AUDIO - FRAME) // STEP
NFFT = FRAME // 2 + 1
NPOW = FRAME
NMEL, NMFCC, DIM = 40, 13, 192
NY = NMFCC + 1
NL = 3 * NMEL
KP = NL + 2
HW = DIM + NY
HEADS, DH, M = 12, 16, 64
HH = HEADS // 2
NE, HD = 3, 64
NH = 32
FW = 3 * DIM + NH
SP = S + 1
KT = DIM // 2
G = 4
NG = BATCH // G
LN_EPS = 1e-5
LOG_EPS = 1e-6
LN_1E4 = 9.210340371976184
NEG = -1e30

PAIRS = [(0, 0), (0, 1), (0, 2), (1, 0), (1, 1), (2, 0)]
KY = len(PAIRS) * NY
KB = 3 * HEADS
KZ = KY + KB
ZW = 2 * KZ


def audio_tower(nc, ins, out):
    fp32, bf16, f32r = mybir.dt.float32, mybir.dt.bfloat16, mybir.dt.float32r
    ALU, ACT, AX = mybir.AluOpType, mybir.ActivationFunctionType, mybir.AxisListType.X
    ctx = ExitStack()

    def sb(name, shape, dt=fp32):
        return ctx.enter_context(nc.sbuf_tensor(name, shape, dt))

    def sem(name):
        return ctx.enter_context(nc.semaphore(name))

    with ctx:
        dft = sb("dft", [FRAME, NPOW])
        ident = sb("ident", [128, 128])
        identb = sb("identb", [128, 128], bf16)
        causalb = sb("causalb", [S, NE, S], bf16)
        ones = sb("ones", [128, 128])
        onesb = sb("onesb", [128, 128], bf16)
        bd = sb("bd", [128, 2])
        log_eps = sb("log_eps", [128, 1])
        neg_half = sb("neg_half", [128, G])
        mel2 = sb("mel2", [NPOW, NL])
        pd = sb("pd", [KP, HW])
        pdh = sb("pdh", [KP, HW], f32r)
        pdr = sb("pdr", [KP, HW], f32r)
        less_e = sb("less_e", [KP, 2])
        w_raw = sb("w_raw", [KY, 2 * DIM], bf16)
        w_q0 = sb("w_q0", [KY, HEADS * M], bf16)
        w_qe = sb("w_qe", [KZ, HEADS * M], bf16)
        w_ke = sb("w_ke", [KZ, HEADS * M], bf16)
        headsb = sb("headsb", [KB, HEADS * M], bf16)
        w_vo = sb("w_vo", [HH * NY, 2, DIM])
        f_w = sb("f_w", [128, 2, FW])
        f_bvg = sb("f_bvg", [3, DIM + NH])
        f_wh = sb("f_wh", [128, 2, FW], f32r)
        f_wl = sb("f_wl", [128, 2, FW], f32r)
        f_bqk = sb("f_bqk", [128, 3])
        f_bparts = sb("f_bparts", [3, DIM + NH], bf16)
        f_wp = sb("f_wp", [KT + 1, 2, DIM])
        f_wg2 = sb("f_wg2", [S, NE, NH + 1])
        less_b = sb("less_b", [3, 2])
        f_cw = sb("f_cw", [HD, 3])
        f_cb = sb("f_cb", [HD, 1])

        h_all = sb("h_all", [S, BATCH, HW])
        zt_all = sb("zt_all", [S, BATCH, ZW], bf16)
        ysT_all = sb("ysT_all", [KY, BATCH, S], bf16)
        y_all = sb("y_all", [S, BATCH, NY])
        yk_all = sb("yk_all", [S, BATCH, 3, NY + 1], bf16)

        xg = [sb(f"xg{i}", [S, G, FRAME]) for i in range(2)]
        x_in = [sem(f"x_in{i}") for i in range(2)]
        frames = ins["x"].rearrange("b (f s) -> f b s", s=STEP)

        own = ExitStack()

        def tmp(name, shape, dt=fp32):
            return own.enter_context(nc.sbuf_tensor(name, shape, dt))

        heads = tmp("heads", [KB, HEADS * M])
        less_q = tmp("less_q", [KZ, 2])
        less_k = tmp("less_k", [KZ, 2])
        blk = tmp("blk", [KT, HH * NY])
        causal = tmp("causal", [S, S])
        dctx = tmp("dctx", [NY, KP])
        wpb = tmp("wpb", [NY, DIM])
        wpc = tmp("wpc", [NY, DIM])
        wrow = tmp("wrow", [NY, 2])
        wpcT = tmp("wpcT", [KT, 2, NY])
        wpcT6 = tmp("wpcT6", [KT, 2, KY])
        wqk_a = tmp("wqk_a", [KT, 2, 2 * DIM])
        wv_a = tmp("wv_a", [KT, 2, DIM])
        wo_a = tmp("wo_a", [KT, 2, DIM])
        projb = tmp("projb", [KT, HH * M])
        a6 = tmp("a6", [KT, 4, KB + KY + KB])
        avT = tmp("avT", [KT, 2, HH * NY])
        part = [[tmp(f"part{p}{i}", [KZ, HH * M], bf16) for i in range(2)] for p in range(2)]
        rest = [tmp(f"rest{i}", [KZ, HH * M]) for i in range(2)]

        bank = [ctx.enter_context(nc.psum_tensor(f"bank{i}", [128, 512], fp32)) for i in range(8)]

        w_in = sem("w_in")
        s_pe, s_dve, s_pool = sem("s_pe"), sem("s_dve"), sem("s_pool")
        first = [
            (wpb[:, :], ins["wpb"]), (dctx[:, :], ins["dctx"]), (ident[:, :], ins["ident"]),
            (wqk_a[:, :, 0:DIM], ins["wq"].rearrange("(t p) n -> p t n", t=2)),
            (wqk_a[:, :, DIM:2 * DIM], ins["wk"].rearrange("(t p) n -> p t n", t=2)),
            (wv_a[:, :, :], ins["wv"].rearrange("(t p) n -> p t n", t=2)),
            (blk[:, :], ins["blk"]), (projb[:, :], ins["projb"]),
            (wo_a[:, :, :], ins["wo"].rearrange("(t p) n -> p t n", t=2)),
            (less_q[:, :], ins["less_q"]), (less_k[:, :], ins["less_k"]), (heads[:, :], ins["heads"]),
        ]
        later = [
            (dft[:, :], ins["dft"]), (mel2[:, :], ins["mel2"]), (pd[:, DIM:HW], ins["dctxT"]), (less_e[:, :], ins["less_e"]),
            (bd[:, :], ins["bd"]), (causal[:, :], ins["causal"]),
            (f_w[:, 0, :], ins["f_w"][0:128, :]), (f_w[0:64, 1, :], ins["f_w"][128:DIM, :]),
            (f_w[64:128, 1, :], ins["f_w"][128:DIM, :]), (f_bqk[:, :], ins["f_bqk"]),
            (f_bvg[:, :], ins["f_bvg"].broadcast_to([3, DIM + NH])),
            (f_wp[0:KT, :, :], ins["f_wp"].rearrange("(t p) n -> p t n", t=2)),
            (f_wp[KT:KT + 1, 1, :], ins["f_bp"]),
            (f_wg2[:, :, :].rearrange("p e n -> p (e n)"), ins["f_wg2"].broadcast_to([S, NE * (NH + 1)])),
            (less_b[:, :], ins["less_b"]), (f_cw[:, :], ins["f_cw"]), (f_cb[:, :], ins["f_cb"]),
        ]
        loads = first + later
        def rep(x, lo, n):
            return a6[:, x, lo:lo + n]

        chunks = [(w_raw, slice(0, 2 * DIM), KY, less_k, [(wpcT6[:, t, :], wqk_a[:, t, :]) for t in range(2)])]
        for half in range(2):
            cols = slice(half * HH * M, (half + 1) * HH * M)
            chunks.append((w_q0, cols, KY, less_k, [(rep(half, KB, KY), projb[:, :])]))
            chunks.append((w_ke, cols, KY, less_k, [(rep(2 + half, KB, KY), projb[:, :])]))
            chunks.append((w_qe, cols, KZ, less_q, [(rep(half, 0, KZ), projb[:, :])]))
        NC = len(chunks)
        c_pe, c_p0, c_x1, c_p1, c_x2 = sem("c_pe"), sem("c_p0"), sem("c_x1"), sem("c_p1"), sem("c_x2")
        heads_b, heads_in = sem("heads_b"), sem("heads_in")
        w_later = sem("w_later")

        def issue(eng, half):
            for n, (dst, src) in enumerate(loads):
                if n % 2 == half:
                    eng.dma_start(dst, src).then_inc(w_in if n < len(first) else w_later, 16)

        with nc.Block() as block:
            @block.sync
            def _(sp):
                issue(sp, 0)
                for i in range(2):
                    sp.dma_start(xg[i][:, :, :], frames[:, i * G:(i + 1) * G, 0:FRAME]).then_inc(x_in[i], 16)
                sp.wait_ge(heads_b, 1)
                sp.dma_start(w_ke[KY:KZ, :], headsb[:, :]).then_inc(heads_in, 16)
                sp.wait_ge(c_x2, NC)
                sp.dma_start(w_qe[0:KB, :], headsb[:, :]).then_inc(heads_in, 16)

            @block.scalar
            def _(act):
                issue(act, 1)
                for n in range(NC + 1):
                    if n < NC:
                        rows = chunks[n][2]
                        act.wait_ge(c_pe, n + 1)
                        if n >= 2:
                            act.wait_ge(c_x1, n - 1)
                        nc.scalar.activation(part[0][n % 2][0:rows, :], bank[4 + n % 4][0:rows, 0:HH * M], ACT.Copy)\
                            .then_inc(c_p0, 1)
                    if n > 0:
                        c = n - 1
                        rows = chunks[c][2]
                        act.wait_ge(c_x1, c + 1)
                        if c >= 2:
                            act.wait_ge(c_x2, c - 1)
                        nc.scalar.activation(part[1][c % 2][0:rows, :], rest[c % 2][0:rows, :], ACT.Copy).then_inc(c_p1, 1)

            @block.gpsimd
            def _(pool):
                nc.gpsimd.memset(a6[:, :, :], 0.0).then_inc(s_pool, 1)
                nc.gpsimd.memset(yk_all[:, :, :, :], 0.0).then_inc(s_pool, 1)
                pool.wait_ge(s_pool, 2)
                nc.gpsimd.memset(yk_all[:, :, 0, NY:NY + 1], 1.0)
                nc.gpsimd.memset(onesb[:, :], 1.0)
                nc.gpsimd.memset(ones[:, :], 1.0)
                nc.gpsimd.memset(log_eps[:, :], LOG_EPS)
                nc.gpsimd.memset(neg_half[:, :], -0.5)
                pool.wait_ge(w_in, 16 * len(first))
                nc.gpsimd.tensor_copy(headsb[:, :], heads[:, :]).then_inc(heads_b, 1)

            @block.tensor
            def _(pe):
                pe.wait_ge(w_in, 16 * len(first))
                nc.tensor.matmul(bank[0][0:KP, 0:DIM], dctx[:, :], wpb[:, :], start=True, stop=True)\
                    .then_inc(s_pe, 1)
                pe.wait_ge(s_dve, 1)
                for t in range(2):
                    last = nc.tensor.transpose(bank[1][0:KT, t * NY:(t + 1) * NY],
                                               wpc[:, t * KT:(t + 1) * KT], ident[0:NY, 0:NY])
                last.then_inc(s_pe, 1)
                pe.wait_ge(s_dve, 2)
                for n in range(6):
                    w = wv_a if n >= 4 else wqk_a
                    c = (n % 2 if n >= 4 else n) * KT
                    for t in range(2):
                        last = nc.tensor.matmul(bank[2][0:KT, n * NY:(n + 1) * NY], w[:, t, c:c + KT],
                                                wpcT[:, t, :], start=(t == 0), stop=(t == 1))
                last.then_inc(s_pe, 1)
                pe.wait_ge(s_dve, 3)
                for half in range(2):
                    last = nc.tensor.matmul(bank[3][0:HH * NY, half * DIM:(half + 1) * DIM], avT[:, half, :],
                                            wo_a[:, half, :], start=True, stop=True)
                last.then_inc(s_pe, 1)
                for n, (dst, cols, rows, later_rows, terms) in enumerate(chunks):
                    if n >= 4:
                        pe.wait_ge(c_x1, n - 3)
                    for t, (l, r) in enumerate(terms):
                        last = nc.tensor.matmul(bank[4 + n % 4][0:rows, 0:HH * M], l, r, start=(t == 0),
                                                stop=(t == len(terms) - 1))
                    last.then_inc(c_pe, 1)

            @block.vector
            def _(dve):
                link = Chain(dve, sem("setup_chain"))
                dve.wait_ge(w_in, 16 * len(first))
                link(nc.vector.reduce_sum(wrow[:, 0:1], wpb[:, :], AX))
                link(nc.vector.tensor_scalar(wrow[:, 1:2], wrow[:, 0:1], 1.0 / DIM, None, ALU.mult))
                link(nc.vector.tensor_scalar(wpc[:, :], wpb[:, :], wrow[:, 1:2], None, ALU.subtract))
                nc.vector.engine_nop().then_inc(s_dve, 1)
                dve.wait_ge(s_pe, 1)
                link(nc.vector.tensor_copy(pd[:, 0:DIM], bank[0][0:KP, 0:DIM]))
                dve.wait_ge(s_pe, 2)
                link(nc.vector.tensor_copy(wpcT[:, :, :], bank[1][0:KT, 0:2 * NY].rearrange("p (t n) -> p t n", t=2)))
                for t in range(2):
                    link(nc.vector.tensor_copy(
                        wpcT6[:, t, :].rearrange("p (r n) -> p r n", n=NY),
                        wpcT[:, t:t + 1, :].broadcast_to([KT, len(PAIRS), NY])))
                nc.vector.engine_nop().then_inc(s_dve, 1)
                dve.wait_ge(s_pe, 3)
                dve.wait_ge(s_pool, 2)
                for n in range(4):
                    src = bank[2][0:KT, n * NY:(n + 1) * NY].rearrange("p (r n) -> p r n", r=1)
                    link(nc.vector.tensor_scalar(
                        a6[:, n, KB:KB + KY].rearrange("p (r n) -> p r n", n=NY),
                        src.broadcast_to([KT, len(PAIRS), NY]), 0.5, None, ALU.mult))
                for n in range(2):
                    src = bank[2][0:KT, (4 + n) * NY:(5 + n) * NY].rearrange("p (r n) -> p r n", r=1)
                    link(nc.vector.tensor_tensor(
                        avT[:, n, :].rearrange("p (r n) -> p r n", n=NY),
                        src.broadcast_to([KT, HH, NY]), blk[:, :].rearrange("p (r n) -> p r n", n=NY), ALU.mult))
                nc.vector.engine_nop().then_inc(s_dve, 1)
                dve.wait_ge(s_pe, 4)
                link(nc.vector.tensor_copy(w_vo[:, :, :], bank[3][0:HH * NY, 0:2 * DIM].rearrange("p (t n) -> p t n", t=2)))
                nc.vector.engine_nop().then_inc(s_dve, 1)
                for n in range(NC + 1):
                    if n < NC:
                        rows, later_rows = chunks[n][2], chunks[n][3]
                        dve.wait_ge(c_p0, n + 1)
                        if n >= 2:
                            dve.wait_ge(c_x2, n - 1)
                        nc.vector.scalar_tensor_tensor(rest[n % 2][0:rows, :], part[0][n % 2][0:rows, :], later_rows[0:rows, 0:1],
                                                       bank[4 + n % 4][0:rows, 0:HH * M], ALU.mult, ALU.add).then_inc(c_x1, 1)
                    if n > 0:
                        dst, cols, rows, later_rows, _ = chunks[n - 1]
                        dve.wait_ge(c_p1, n)
                        nc.vector.scalar_tensor_tensor(dst[0:rows, cols], part[1][(n - 1) % 2][0:rows, :], later_rows[0:rows, 1:2],
                                                       rest[(n - 1) % 2][0:rows, :], ALU.mult, ALU.add).then_inc(c_x2, 1)
                dve.wait_ge(w_later, 16 * len(later))
                link(nc.vector.tensor_copy(pdh[:, :], pd[:, :]))
                nc.vector.scalar_tensor_tensor(pdr[:, :], pdh[:, :], less_e[:, 1:2], pd[:, :], ALU.mult, ALU.add)
                nc.vector.tensor_copy(identb[:, :], ident[:, :])
                nc.vector.tensor_copy(causalb[:, :, :],
                                      causal[:, :].rearrange("p (e s) -> p e s", e=1).broadcast_to([S, NE, S]))

        own.close()
        tokens(nc, sem, bank, ins, out, locals())
        attention(nc, sem, bank, ins, out, locals())
        ffn(nc, sem, bank, ins, out, locals())


class Chain:
    def __init__(self, eng, done):
        self.eng, self.done, self.count = eng, done, 0

    def __call__(self, instruction):
        self.count += 1
        instruction.then_inc(self.done, 1)
        self.eng.wait_ge(self.done, self.count)


def pipeline(eng, step, items, unroll, skew, peel=0):
    first = -(-max(skew, peel) // unroll)
    for t in range(first * unroll):
        step(t, t % unroll, t // unroll)
    with eng.Fori(first, items // unroll) as i:
        for j in range(unroll):
            step(i * unroll + j, j, i)
    for t in range(items, items + skew):
        step(t, t % unroll, t // unroll)


def there(t, items):
    return not isinstance(t, int) or 0 <= t < items


def due(n):
    return not isinstance(n, int) or n > 0


COUNTS = itertools.count()


@contextmanager
def apart(eng, n):
    if isinstance(n, int):
        yield n
    else:
        with eng.register(f"count{next(COUNTS)}") as r:
            eng.reg_add(r, n, 0)
            yield r


def with_exitstack_sb(phase):
    def run(nc, sem, *rest):
        with ExitStack() as own:
            phase(nc, lambda name, shape, dt=mybir.dt.float32: own.enter_context(nc.sbuf_tensor(name, shape, dt)),
                  sem, *rest)
    return run


@with_exitstack_sb
def tokens(nc, sb, sem, bank, ins, out, v):
    fp32, bf16, f32r = mybir.dt.float32, mybir.dt.bfloat16, mybir.dt.float32r
    ALU, ACT = mybir.AluOpType, mybir.ActivationFunctionType
    ident, identb, dft, mel2, pdr, less_e, ones = (
        v[n] for n in ("ident", "identb", "dft", "mel2", "pdr", "less_e", "ones"))
    h_all, zt_all, ysT_all, y_all, yk_all = v["h_all"], v["zt_all"], v["ysT_all"], v["y_all"], v["yk_all"]
    log_eps, neg_half = v["log_eps"], v["neg_half"]
    heads_in, xg, x_in, frames = v["heads_in"], v["xg"], v["x_in"], v["frames"]
    f_w, f_wh, f_wl, f_bvg, f_bparts, less_b = (v[n] for n in ("f_w", "f_wh", "f_wl", "f_bvg", "f_bparts", "less_b"))
    T = G * S

    xT = [sb(f"xT{i}", [FRAME, T]) for i in range(2)]
    power = [sb(f"power{i}", [NPOW, T]) for i in range(2)]
    logE = [sb(f"logE{i}", [NL, G, S]) for i in range(2)]
    logEh = [sb(f"logEh{i}", [NL, G, S], f32r) for i in range(2)]
    logEp = [sb(f"logEp{i}", [KP, G, SP], f32r) for i in range(2)]
    stats = [sb(f"stats{i}", [S, G, 6]) for i in range(2)]
    mv = [sb(f"mv{i}", [S, G, 2]) for i in range(2)]
    vare = [sb(f"vare{i}", [S, G]) for i in range(2)]
    rstd = [sb(f"rstd{i}", [S, G]) for i in range(2)]
    yrest = sb("yrest", [S, G, NY])
    bp0, bp1 = sb("bp0", [3, DIM + NH], bf16), sb("bp1", [3, DIM + NH], bf16)
    brest = sb("brest", [3, DIM + NH])

    p_xT, p_dft, p_mel, p_hy, p_ysT = (sem(n) for n in ("p_xT", "p_dft", "p_mel", "p_hy", "p_ysT"))
    a_xT, a_pow, a_log, a_h = (sem(n) for n in ("a_xT", "a_pow", "a_log", "a_h"))
    d_stat, d_y, d_ysT, d_var, d_aggr, d_log = (sem(n) for n in ("d_stat", "d_y", "d_ysT", "d_var", "d_aggr", "d_log"))
    g_rstd, g_yk = sem("g_rstd"), sem("g_yk")
    B_XT, B_DFT, B_MEL, B_HY, B_YST = bank[0], bank[1], bank[2], bank[3:5], bank[5]
    SKEW = 7

    def gsl(t):
        return bass.ds(t * G, G)

    with nc.Block() as block:
        @block.sync
        def _(sp):
            with sp.Fori(1, NG // 2) as i:
                for j in range(2):
                    sp.wait_ge(p_xT, 2 * i + j - 1)
                    sp.dma_start(xg[j][:, :, :], frames[:, gsl(2 * i + j), 0:FRAME]).then_inc(x_in[j], 16)
            sp.wait_ge(heads_in, 32)

        @block.tensor
        def _(pe):
            def step(t, j, i):
                if there(t, NG):
                    pe.wait_ge(x_in[j], (t - j) * 8 + 16)
                    if due(t):
                        pe.wait_ge(a_xT, t)
                    for b in range(G):
                        last = nc.tensor.transpose(B_XT[0:FRAME, b * S:(b + 1) * S], xg[j][:, b, :], ident[0:S, 0:S])
                    last.then_inc(p_xT, 1)
                if there(t - 1, NG):
                    if due(t):
                        pe.wait_ge(a_xT, t)
                    if due(t - 1):
                        pe.wait_ge(a_pow, t - 1)
                    nc.tensor.matmul(B_DFT[0:NPOW, 0:T], dft[:, :], xT[1 - j][:, :], start=True, stop=True)\
                        .then_inc(p_dft, 1)
                if there(t - 2, NG):
                    if due(t - 1):
                        pe.wait_ge(a_pow, t - 1)
                    if due(t - 2):
                        pe.wait_ge(a_log, t - 2)
                    nc.tensor.matmul(B_MEL[0:NL, 0:T], mel2[:, :], power[j][:, :], start=True, stop=True)\
                        .then_inc(p_mel, 1)
                if there(t - 3, NG):
                    if due(t - 2):
                        pe.wait_ge(d_log, t - 2)
                    if due(t - 3):
                        pe.wait_ge(a_h, t - 3)
                    for b in range(G):
                        last = nc.tensor.matmul(B_HY[b // 2][0:S, (b % 2) * HW:(b % 2 + 1) * HW],
                                                logEp[1 - j][:, b, 0:S], pdr[:, :], start=True, stop=True)
                    last.then_inc(p_hy, 1)
                if there(t - 6, NG):
                    if due(5 * (t - 5)):
                        pe.wait_ge(d_y, 5 * (t - 5))
                    if due(t - 6):
                        pe.wait_ge(d_ysT, t - 6)
                    for b in range(G):
                        last = nc.tensor.matmul(B_YST[0:KY, b * S:(b + 1) * S], zt_all[:, (t - 6) * G + b, KB:KB + KY],
                                                identb[0:S, 0:S], start=True, stop=True)
                    last.then_inc(p_ysT, 1)
            pipeline(pe, step, NG, 2, SKEW)

        @block.scalar
        def _(act):
            def step(t, j, i):
                if there(t, NG):
                    act.wait_ge(p_xT, t + 1)
                    if due(t - 1):
                        act.wait_ge(p_dft, t - 1)
                    nc.scalar.activation(xT[j][:, :], B_XT[0:FRAME, 0:T], ACT.Copy).then_inc(a_xT, 1)
                if there(t - 1, NG):
                    if due(t):
                        act.wait_ge(p_dft, t)
                    if due(t - 2):
                        act.wait_ge(p_mel, t - 2)
                    nc.scalar.activation(power[1 - j][:, :], B_DFT[0:NPOW, 0:T], ACT.Square).then_inc(a_pow, 1)
                if there(t - 2, NG):
                    if due(t - 1):
                        act.wait_ge(p_mel, t - 1)
                    if due(t - 3):
                        act.wait_ge(d_log, t - 3)
                    for x in (logE, logEh):
                        last = nc.scalar.activation(x[j][:, :, :], B_MEL[0:NL, 0:T].rearrange("p (b s) -> p b s", b=G), ACT.Ln,
                                                    bias=log_eps[0:NL, :])
                    last.then_inc(a_log, 1)
                if there(t - 3, NG):
                    if due(t - 2):
                        act.wait_ge(p_hy, t - 2)
                    for half in range(2):
                        last = nc.scalar.activation(
                            h_all[:, bass.ds((t - 3) * G + 2 * half, 2), :],
                            B_HY[half][0:S, 0:2 * HW].rearrange("p (b n) -> p b n", b=2), ACT.Copy)
                    last.then_inc(a_h, 1)
            pipeline(act, step, NG, 2, SKEW)

        @block.gpsimd
        def _(pool):
            def step(t, j, i):
                if there(t - 4, NG):
                    u = j
                    if due(t - 3):
                        with apart(pool, t - 3) as count:
                            pool.wait_ge(d_var, 1)
                            pool.wait_ge(d_var, count)
                    nc.gpsimd.tensor_tensor(rstd[u][:, :], vare[u][:, :], neg_half[0:S, :], ALU.pow).then_inc(g_rstd, 1)
                if there(t - 6, NG):
                    z = zt_all[:, gsl(t - 6), KB:KB + KY].rearrange("p b (r n) -> p b r n", n=NY)
                    if due(5 * (t - 5)):
                        with apart(pool, 5 * (t - 5)) as count:
                            pool.wait_ge(d_y, 1)
                            pool.wait_ge(d_y, count)
                    nc.gpsimd.tensor_copy(yk_all[:, gsl(t - 6), :, 0:NY], z[:, :, 1::2, :]).then_inc(g_yk, 1)
            pipeline(pool, step, NG, 2, SKEW)

        @block.vector
        def _(dve):
            def step(t, j, i):
                u = 1 - j
                if there(t - 3, NG):
                    if due(t - 2):
                        dve.wait_ge(a_log, t - 2)
                    if due(t - 4):
                        dve.wait_ge(p_hy, t - 4)
                    nc.vector.scalar_tensor_tensor(logEp[u][0:NL, :, 0:S], logEh[u][:, :, :], less_e[0:NL, 0:1],
                                                   logE[u][:, :, :], ALU.mult, ALU.add).then_inc(d_log, 1)
                v, c = t - 4, t - 5
                if there(c, NG):
                    y = y_all[:, gsl(c), :]
                    y4 = y_all[:, gsl(c), :].rearrange("p b (r n) -> p b r n", r=1)
                    r4 = yrest[:, :, :].rearrange("p b (r n) -> p b r n", r=1)
                    z = zt_all[:, gsl(c), KB:KB + KY].rearrange("p b (r n) -> p b r n", n=NY)

                def moments(b):
                    return nc.vector.bn_stats(stats[j][:, b, :], h_all[:, v * G + b, 0:DIM])

                if there(v, NG):
                    dve.wait_ge(a_h, v + 1)
                    moments(0)
                if there(c, NG):
                    dve.wait_ge(g_rstd, c + 1)
                    nc.vector.tensor_tensor(y, h_all[:, gsl(c), DIM:HW],
                                            rstd[1 - j][:, :].rearrange("p (b n) -> p b n", n=1).broadcast_to([S, G, NY]),
                                            ALU.mult).then_inc(d_y, 1)
                if there(v, NG):
                    moments(1)
                if there(c, NG):
                    dve.wait_ge(d_y, 5 * c + 1)
                    nc.vector.tensor_copy(z[:, :, 0:3, :], y4.broadcast_to([S, G, 3, NY])).then_inc(d_y, 1)
                if there(v, NG):
                    moments(2)
                if there(c, NG):
                    dve.wait_ge(d_y, 5 * c + 2)
                    nc.vector.tensor_tensor(yrest[:, :, :], y, z[:, :, 0, :], ALU.subtract).then_inc(d_y, 1)
                if there(v, NG):
                    moments(3).then_inc(d_stat, 1)
                if there(c, NG):
                    dve.wait_ge(d_y, 5 * c + 3)
                    nc.vector.tensor_copy(z[:, :, 3:5, :], r4.broadcast_to([S, G, 2, NY])).then_inc(d_y, 1)
                if there(v, NG):
                    with apart(dve, v + 1) as count:
                        dve.wait_ge(d_stat, 1)
                        dve.wait_ge(d_stat, count)
                    for b in range(G):
                        last = nc.vector.bn_aggr(mv[j][:, b, :], stats[j][:, b, :])
                    last.then_inc(d_aggr, 1)
                if there(c, NG):
                    dve.wait_ge(d_y, 5 * c + 4)
                    nc.vector.tensor_tensor(z[:, :, 5, :], yrest[:, :, :], z[:, :, 3, :], ALU.subtract).then_inc(d_y, 1)
                if there(v, NG):
                    dve.wait_ge(d_aggr, v + 1)
                    if due(v - 1):
                        dve.wait_ge(g_rstd, v - 1)
                    nc.vector.tensor_scalar(vare[j][:, :], mv[j][:, :, 1], LN_EPS, None, ALU.add).then_inc(d_var, 1)
                if there(t - 6, NG):
                    if due(t - 5):
                        dve.wait_ge(p_ysT, t - 5)
                    nc.vector.tensor_copy(ysT_all[:, gsl(t - 6), :],
                                          B_YST[0:KY, 0:T].rearrange("p (b n) -> p b n", b=G)).then_inc(d_ysT, 1)

            link = Chain(dve, sem("f_parts"))
            for i in range(2):
                link(nc.vector.tensor_copy(
                    logEp[i][:, :, :], ones[0:KP, 0:SP].rearrange("p (b s) -> p b s", b=1).broadcast_to([KP, G, SP])))
            link(nc.vector.tensor_copy(f_wh[:, :, :], f_w[:, :, :]))
            link(nc.vector.tensor_tensor(f_wl[:, :, :], f_w[:, :, :], f_wh[:, :, :], ALU.subtract))
            link(nc.vector.tensor_copy(bp0[:, :], f_bvg[:, :]))
            link(nc.vector.scalar_tensor_tensor(brest[:, :], bp0[:, :], less_b[:, 0:1], f_bvg[:, :], ALU.mult, ALU.add))
            link(nc.vector.tensor_copy(bp1[:, :], brest[:, :]))
            link(nc.vector.scalar_tensor_tensor(f_bparts[:, :], bp1[:, :], less_b[:, 1:2], brest[:, :], ALU.mult, ALU.add))
            pipeline(dve, step, NG, 2, SKEW)


@with_exitstack_sb
def attention(nc, sb, sem, bank, ins, out, v):
    fp32, bf16 = mybir.dt.float32, mybir.dt.bfloat16
    ALU, ACT, AX = mybir.AluOpType, mybir.ActivationFunctionType, mybir.AxisListType.X
    ident, identb, ones = v["ident"], v["identb"], v["ones"]
    w_raw, w_q0, w_qe, w_ke, w_vo = v["w_raw"], v["w_q0"], v["w_qe"], v["w_ke"], v["w_vo"]
    h_all, zt_all, ysT_all, yk_all, onesb, bd = (v[n] for n in ("h_all", "zt_all", "ysT_all", "yk_all", "onesb", "bd"))
    f16 = mybir.dt.float16
    HALF = HH * M
    R1 = NY + 1

    mx_all = sb("mx_all", [S, BATCH, 2 * HEADS])
    dg_all = sb("dg_all", [S, BATCH, 2 * HEADS])
    mxk = sb("mxk", [S, G * HEADS])
    stab = sb("stab", [G * HEADS, 1])
    stabd = sb("stabd", [G * HEADS, G * HEADS])
    off0 = sb("off0", [S, G, 2 * HEADS])
    off = sb("off", [S, G, 2, HEADS])
    orest = sb("orest", [S, G, 2, HEADS])
    sq = [sb(f"sq{i}", [S, 2 * DIM]) for i in range(2)]
    zT = [sb(f"zT{i}", [KZ, 2, S], bf16) for i in range(2)]
    kf = [sb(f"kf{i}", [S, HEADS * M]) for i in range(2)]
    kh = [sb(f"kh{i}", [S, HEADS * M], f16) for i in range(2)]
    kl = [sb(f"kl{i}", [S, HEADS * M], f16) for i in range(2)]
    qf = [sb(f"qf{i}", [128, HH, S]) for i in range(2)]
    qh = [sb(f"qh{i}", [128, HH, 128], f16) for i in range(4)]
    ql = [sb(f"ql{i}", [128, HH, 128], f16) for i in range(4)]
    csum = sb("csum", [128, HH * R1])
    cbd = [sb(f"cbd{i}", [128, HH, 2, R1]) for i in range(2)]
    crest = [sb(f"crest{i}", [128, HH, 2, R1]) for i in range(2)]
    cpart = [[sb(f"cpart{p}{i}", [128, HH, 2, R1], bf16) for p in range(3)] for i in range(4)]
    rden = [sb(f"rden{i}", [S, HEADS]) for i in range(2)]
    rn = [sb(f"rn{i}", [S, HEADS * NY]) for i in range(2)]
    rnT = [sb(f"rnT{i}", [HH * NY, 2, S]) for i in range(2)]

    names = ["raw", "dash", "mxT", "stab", "z", "ek", "eq", "ctx", "num", "numT", "proj"]
    p = {n: sem(f"p_{n}") for n in names}
    a = {n: sem(f"a_{n}") for n in ("sq", "ek", "eq", "z", "c1", "c2", "numT")}
    d = {n: sem(f"d_{n}") for n in ("dg", "max", "mxk", "stab", "off", "csum", "cbd", "crest", "ql", "rden", "num", "h")}
    g = {n: sem(f"g_{n}") for n in ("kl", "ql", "c3", "off", "zero")}
    B_RAW, B_M, B_X, B_T, B_C, B_R = bank[0], bank[1:3], bank[3:5], bank[5], bank[6], bank[7]
    QD = 3
    Z, KQ, CT, NU, TR, PR = 6, 7, 8, 10, 11, 12

    with nc.Block() as block:
        @block.tensor
        def _(pe):
            pe.wait_ge(g["zero"], 8)

            def dash(t, c):
                w = (w_q0, w_ke)[c // 2]
                if due(4 * t + c - 1):
                    pe.wait_ge(d["max"], 4 * t + c - 1)
                nc.tensor.matmul(B_M[c % 2][0:S, 0:HALF], ysT_all[:, t, :], w[0:KY, (c % 2) * HALF:(c % 2 + 1) * HALF],
                                 start=True, stop=True).then_inc(p["dash"], 1)

            def step(t, j, i):
                if there(t, BATCH):
                    dash(t, 0)
                    dash(t, 1)
                    if due(t):
                        pe.wait_ge(a["sq"], t)
                    if due(t - PR):
                        pe.wait_ge(d["h"], t - PR)
                    nc.tensor.matmul(B_RAW[0:S, 0:2 * DIM], ysT_all[:, t, :], w_raw[:, :], start=True, stop=True)\
                        .then_inc(p["raw"], 1)
                b = t - KQ
                if there(b, BATCH):
                    pe.wait_ge(a["z"], b + 1)
                    for half in range(2):
                        if due(2 * b - 1 + half):
                            pe.wait_ge(a["eq"], 2 * b - 1 + half)
                        nc.tensor.matmul(B_X[half][0:S, 0:HALF], zT[(j - KQ) % 2][:, 1, :],
                                         w_ke[:, half * HALF:(half + 1) * HALF], start=True, stop=True)\
                            .then_inc(p["ek"], 1)
                b = t - Z
                if there(b, BATCH):
                    pe.wait_ge(g["off"], b - (j - Z) % G + G)
                    if due(b):
                        pe.wait_ge(a["z"], b)
                    if j == 0 and there(t - 4, BATCH):
                        if due(2 * i - 1):
                            pe.wait_ge(d["stab"], 2 * i - 1)
                    if j == 1 and there(t - 5, BATCH):
                        if due(3 * i):
                            pe.wait_ge(d["off"], 3 * i)
                    for n, lo in enumerate((0, KB)):
                        last = nc.tensor.matmul(B_T[0:KZ, n * S:(n + 1) * S], zt_all[:, b, lo:lo + KZ], identb[0:S, 0:S],
                                                start=True, stop=True)
                    last.then_inc(p["z"], 1)
                if there(t, BATCH):
                    dash(t, 2)
                    dash(t, 3)
                b = t - CT
                if there(b, BATCH):
                    pe.wait_ge(g["kl"], b + 1)
                    if due(b - 3):
                        pe.wait_ge(a["numT"], b - 3)
                    y = yk_all[:, bass.ds(b, 1), :, :].rearrange("p b r n -> p b (r n)")
                    nc.tensor.matmul(B_C[:, 0:HH * 3 * R1], onesb[0:S, :], y.broadcast_to([S, HH, 3 * R1]),
                                     start=True, stop=False, skip_group_check=True)
                    for n in range(HH):
                        for x in (kh, kl):
                            last = nc.tensor.matmul(B_C[:, n * 3 * R1:(n + 1) * 3 * R1],
                                                    x[(j - CT) % 2][:, n * 128:(n + 1) * 128], y[:, 0, :],
                                                    start=False, stop=(x is kl), skip_group_check=True)
                    last.then_inc(p["ctx"], 1)
                b = t - KQ
                if there(b, BATCH):
                    for half in range(2):
                        pe.wait_ge(a["ek"], 2 * b + 1 + half)
                        for n in range(3):
                            f = (3 * half + n) * 128
                            last = nc.tensor.matmul(B_X[half][:, n * S:(n + 1) * S], w_qe[:, f:f + 128],
                                                    zT[(j - KQ) % 2][:, 0, :], start=True, stop=True)
                        last.then_inc(p["eq"], 1)
                b = t - NU
                if there(b, BATCH):
                    pe.wait_ge(d["ql"], b + 1)
                    pe.wait_ge(g["ql"], b + 1)
                    pe.wait_ge(g["c3"], b + 1)
                    if due(b):
                        pe.wait_ge(d["num"], b)
                    c = cpart[(j - NU) % 4]
                    for r in range(3):
                        nc.tensor.matmul(B_R[:, 0:HH * 2 * R1], onesb[:, :], c[r][:, :, :, :].rearrange("p n w r -> p (n w r)"),
                                         start=(r == 0), stop=False, skip_group_check=True)
                    for n in range(HH):
                        for x in (qh, ql):
                            for r in range(3):
                                last = nc.tensor.matmul(B_R[:, n * 2 * R1:(n + 1) * 2 * R1], x[(j - NU) % 4][:, n, :],
                                                        c[r][:, n, :, :].rearrange("p w r -> p (w r)"), start=False,
                                                        stop=(x is ql and r == 2), skip_group_check=True)
                    last.then_inc(p["num"], 1)
                b = t - TR
                if there(b, BATCH):
                    pe.wait_ge(d["num"], b + 1)
                    if there(t - CT, BATCH):
                        pe.wait_ge(d["csum"], t - CT + 1)
                    else:
                        if due(b):
                            pe.wait_ge(a["numT"], b)
                    for n in range(2):
                        last = nc.tensor.transpose(B_C[0:HH * NY, n * S:(n + 1) * S],
                                                   rn[(j - TR) % 2][:, n * HH * NY:(n + 1) * HH * NY], ident[0:S, 0:S])
                    last.then_inc(p["numT"], 1)
                b = t - PR
                if there(b, BATCH):
                    pe.wait_ge(a["numT"], b + 1)
                    pe.wait_ge(a["sq"], t + 1 if there(t, BATCH) else BATCH)
                    if due(b):
                        pe.wait_ge(d["h"], b)
                    for n in range(2):
                        last = nc.tensor.matmul(B_RAW[0:S, 0:DIM], rnT[(j - PR) % 2][:, n, :], w_vo[:, n, :],
                                                start=(n == 0), stop=(n == 1))
                    last.then_inc(p["proj"], 1)
                if j == 3 and there(t, BATCH):
                    if there(t - Z, BATCH):
                        pe.wait_ge(a["z"], t - Z + 1)
                    with apart(pe, i + 1) as count:
                        pe.wait_ge(d["mxk"], 1)
                        pe.wait_ge(d["mxk"], count)
                    nc.tensor.transpose(B_T[0:G * HEADS, 0:S], mxk[:, :], ident[0:S, 0:S]).then_inc(p["mxT"], 1)
                if j == 0 and there(t - 4, BATCH):
                    if due(2 * i):
                        pe.wait_ge(d["stab"], 2 * i)
                    if there(t - Z, BATCH):
                        pe.wait_ge(a["z"], t - Z + 1)
                    nc.tensor.matmul(B_T[0:S, 0:G * HEADS], ones[0:G * HEADS, 0:S], stabd[:, :], start=True, stop=True)\
                        .then_inc(p["stab"], 1)
            pipeline(pe, step, BATCH, 4, PR, peel=PR + 1)

        @block.scalar
        def _(act):
            def step(t, j, i):
                if there(t, BATCH):
                    act.wait_ge(p["raw"], t + 1)
                    if due(t - 1):
                        act.wait_ge(d["dg"], t - 1)
                    nc.scalar.activation(sq[j % 2][:, :], B_RAW[0:S, 0:2 * DIM], ACT.Square, scale=0.5).then_inc(a["sq"], 1)
                b = t - KQ
                if there(b, BATCH):
                    if due(b - 1):
                        act.wait_ge(p["ctx"], b - 1)
                    for half in range(2):
                        act.wait_ge(p["ek"], 2 * b + 1 + half)
                        for x in (kf, kh):
                            last = nc.scalar.activation(x[(j - KQ) % 2][:, half * HALF:(half + 1) * HALF],
                                                        B_X[half][0:S, 0:HALF], ACT.Exp)
                        last.then_inc(a["ek"], 1)
                b = t - Z
                if there(b, BATCH):
                    act.wait_ge(p["z"], b + 1)
                    if due(2 * (b - 1)):
                        act.wait_ge(p["eq"], 2 * (b - 1))
                    nc.scalar.activation(zT[(j - Z) % 2][:, :, :], B_T[0:KZ, 0:2 * S].rearrange("p (n s) -> p n s", n=2),
                                         ACT.Copy).then_inc(a["z"], 1)
                b = t - KQ
                if there(b, BATCH):
                    if due(b - 3):
                        act.wait_ge(p["num"], b - 3)
                    if due(b - 1):
                        act.wait_ge(d["ql"], b - 1)
                    if due(b - 1):
                        act.wait_ge(g["ql"], b - 1)
                    for half in range(2):
                        act.wait_ge(p["eq"], 2 * b + 1 + half)
                        for x in (qf[(j - KQ) % 2][:, 3 * half:3 * half + 3, :], qh[(j - KQ) % 4][:, 3 * half:3 * half + 3, 0:S]):
                            last = nc.scalar.activation(x, B_X[half][:, 0:3 * S].rearrange("p (n s) -> p n s", n=3), ACT.Exp)
                        last.then_inc(a["eq"], 1)
                for b, n, src, made, done in ((t - CT, 0, cbd, d["cbd"], a["c1"]), (t - CT - 1, 1, crest, d["crest"], a["c2"])):
                    if there(b, BATCH):
                        act.wait_ge(made, b + 1)
                        if due(b - 3):
                            act.wait_ge(p["num"], b - 3)
                        nc.scalar.activation(cpart[(j - CT - n) % 4][n][:, :, :, :], src[(j - CT - n) % 2][:, :, :, :], ACT.Copy)\
                            .then_inc(done, 1)
                b = t - TR
                if there(b, BATCH):
                    act.wait_ge(p["numT"], b + 1)
                    if due(b - 1):
                        act.wait_ge(p["proj"], b - 1)
                    nc.scalar.activation(rnT[(j - TR) % 2][:, :, :], B_C[0:HH * NY, 0:2 * S].rearrange("p (n s) -> p n s", n=2),
                                         ACT.Copy).then_inc(a["numT"], 1)
            pipeline(act, step, BATCH, 4, PR, peel=PR + 1)

        @block.vector
        def _(dve):
            def step(t, j, i):
                if j == 0 and there(t - 4, BATCH):
                    if due(i):
                        dve.wait_ge(p["mxT"], i)
                    nc.vector.reduce_max(stab[:, :], B_T[0:G * HEADS, 0:S], AX).then_inc(d["stab"], 1)
                    if due(2 * i - 1):
                        dve.wait_ge(d["stab"], 2 * i - 1)
                    nc.vector.tensor_scalar(stabd[:, :], ident[0:G * HEADS, 0:G * HEADS], stab[:, 0:1], None, ALU.mult)\
                        .then_inc(d["stab"], 1)
                if j == 1 and there(t - 5, BATCH):
                    grp = bass.ds(t - 5, G)
                    if due(t - 5):
                        dve.wait_ge(g["off"], t - 5)
                    nc.vector.tensor_scalar(off0[:, :, :], dg_all[:, grp, :], -0.5, LN_1E4, ALU.mult, ALU.add)\
                        .then_inc(d["off"], 1)
                    if due(3 * i - 2):
                        dve.wait_ge(d["off"], 3 * i - 2)
                    nc.vector.tensor_tensor(off[:, :, 0, :], off0[:, :, 0:HEADS], mx_all[:, grp, 0:HEADS], ALU.subtract)\
                        .then_inc(d["off"], 1)
                    if due(i):
                        dve.wait_ge(p["stab"], i)
                    nc.vector.tensor_tensor(off[:, :, 1, :], off0[:, :, HEADS:2 * HEADS],
                                            B_T[0:S, 0:G * HEADS].rearrange("p (b h) -> p b h", b=G), ALU.subtract)\
                        .then_inc(d["off"], 1)
                b = t - CT - 1
                if there(b, BATCH):
                    u = (j - CT - 1) % 2
                    if due(b - 1):
                        dve.wait_ge(g["c3"], b - 1)
                    dve.wait_ge(a["c1"], b + 1)
                    nc.vector.tensor_tensor(crest[u][:, :, :, :], cbd[u][:, :, :, :], cpart[(j - CT - 1) % 4][0][:, :, :, :],
                                            ALU.subtract).then_inc(d["crest"], 1)
                if there(t, BATCH):
                    for c in range(4):
                        dve.wait_ge(p["dash"], 4 * t + 1 + c)
                        nc.vector.reduce_max(mx_all[:, t, c * HH:(c + 1) * HH],
                                             B_M[c % 2][0:S, 0:HALF].rearrange("p (h m) -> p h m", m=M), AX)\
                            .then_inc(d["max"], 1)
                    dve.wait_ge(a["sq"], t + 1)
                    nc.vector.reduce_sum(dg_all[:, t, :], sq[j % 2][:, :].rearrange("p (h d) -> p h d", d=DH), AX)\
                        .then_inc(d["dg"], 1)
                if j == 3 and there(t, BATCH):
                    with apart(dve, 4 * t + 4) as count:
                        dve.wait_ge(d["max"], 1)
                        dve.wait_ge(d["max"], count)
                    if due(i):
                        dve.wait_ge(p["mxT"], i)
                    nc.vector.tensor_copy(mxk[:, :].rearrange("p (b h) -> p b h", b=G),
                                          mx_all[:, bass.ds(t - 3, G), HEADS:2 * HEADS]).then_inc(d["mxk"], 1)
                b = t - CT
                if there(b, BATCH):
                    dve.wait_ge(p["ctx"], b + 1)
                    nc.vector.reduce_sum(csum[:, :].rearrange("p (n r) -> p n r", n=HH),
                                         B_C[:, 0:HH * 3 * R1].rearrange("p (n w r) -> p n r w", n=HH, w=3), AX)\
                        .then_inc(d["csum"], 1)
                    dve.wait_ge(d["csum"], b + 1)
                    if due(b - 1):
                        dve.wait_ge(a["c1"], b - 1)
                    nc.vector.tensor_tensor(cbd[(j - CT) % 2][:, :, :, :],
                                            csum[:, :].rearrange("p (n w r) -> p n w r", n=HH, w=1).broadcast_to([128, HH, 2, R1]),
                                            bd[:, :].rearrange("p (n w r) -> p n w r", n=1, r=1).broadcast_to([128, HH, 2, R1]),
                                            ALU.mult).then_inc(d["cbd"], 1)
                b = t - NU
                if there(b, BATCH):
                    u = (j - NU) % 2
                    num = B_R[0:S, 0:HEADS * R1].rearrange("p (h r) -> p h r", h=HEADS)
                    dve.wait_ge(p["num"], b + 1)
                    nc.vector.reciprocal(rden[u][:, :], num[:, :, NY]).then_inc(d["rden"], 1)
                    dve.wait_ge(d["rden"], b + 1)
                    if due(b - 1):
                        dve.wait_ge(p["numT"], b - 1)
                    nc.vector.tensor_tensor(rn[u][:, :].rearrange("p (h r) -> p h r", h=HEADS), num[:, :, 0:NY],
                                            rden[u][:, :].rearrange("p (h r) -> p h r", r=1).broadcast_to([S, HEADS, NY]),
                                            ALU.mult).then_inc(d["num"], 1)
                b = t - KQ
                if there(b, BATCH):
                    dve.wait_ge(a["eq"], 2 * b + 2)
                    if due(b - 3):
                        dve.wait_ge(p["num"], b - 3)
                    nc.vector.tensor_tensor(ql[(j - KQ) % 4][:, 0:QD, 0:S], qf[(j - KQ) % 2][:, 0:QD, :],
                                            qh[(j - KQ) % 4][:, 0:QD, 0:S], ALU.subtract).then_inc(d["ql"], 1)
                b = t - PR
                if there(b, BATCH):
                    dve.wait_ge(p["proj"], b + 1)
                    nc.vector.tensor_tensor(h_all[:, b, 0:DIM], B_RAW[0:S, 0:DIM], h_all[:, b, 0:DIM], ALU.add)\
                        .then_inc(d["h"], 1)
            pipeline(dve, step, BATCH, 4, PR, peel=PR + 1)

        @block.gpsimd
        def _(pool):
            for i in range(4):
                nc.gpsimd.memset(qh[i][:, :, S:128], 0.0).then_inc(g["zero"], 1)
                nc.gpsimd.memset(ql[i][:, :, S:128], 0.0).then_inc(g["zero"], 1)

            def step(t, j, i):
                b = t - CT - 2
                if there(b, BATCH):
                    with apart(pool, b + 1) as count:
                        if due(b - 3):
                            pool.wait_ge(p["num"], b - 3)
                        pool.wait_ge(a["c2"], 1)
                        pool.wait_ge(a["c2"], count)
                    nc.gpsimd.tensor_tensor(cpart[(j - CT - 2) % 4][2][:, :, :, :], crest[(j - CT) % 2][:, :, :, :],
                                            cpart[(j - CT - 2) % 4][1][:, :, :, :], ALU.subtract).then_inc(g["c3"], 1)
                if j == 1 and there(t - 5, BATCH):
                    c = t - 5
                    z = zt_all[:, bass.ds(c, G), :].rearrange("p b (w c) -> p b w c", w=2)
                    if due(3 * i):
                        with apart(pool, 3 * i) as count:
                            pool.wait_ge(d["off"], 1)
                            pool.wait_ge(d["off"], count)
                    nc.gpsimd.tensor_copy(z[:, :, :, 0:HEADS], off[:, :, :, :]).then_inc(g["off"], 1)
                    with apart(pool, c + 1) as count:
                        pool.wait_ge(g["off"], 1)
                        pool.wait_ge(g["off"], count)
                    nc.gpsimd.tensor_tensor(orest[:, :, :, :], off[:, :, :, :], z[:, :, :, 0:HEADS], ALU.subtract)\
                        .then_inc(g["off"], 1)
                    with apart(pool, c + 2) as count:
                        pool.wait_ge(g["off"], 1)
                        pool.wait_ge(g["off"], count)
                    nc.gpsimd.tensor_copy(z[:, :, :, HEADS:2 * HEADS], orest[:, :, :, :]).then_inc(g["off"], 1)
                    with apart(pool, c + 3) as count:
                        pool.wait_ge(g["off"], 1)
                        pool.wait_ge(g["off"], count)
                    nc.gpsimd.tensor_tensor(z[:, :, :, 2 * HEADS:3 * HEADS], orest[:, :, :, :],
                                            z[:, :, :, HEADS:2 * HEADS], ALU.subtract).then_inc(g["off"], 1)
                b = t - KQ
                if there(b, BATCH):
                    with apart(pool, 2 * b + 2) as count:
                        if due(b - 1):
                            pool.wait_ge(p["ctx"], b - 1)
                        pool.wait_ge(a["ek"], 1)
                        pool.wait_ge(a["ek"], count)
                    nc.gpsimd.tensor_tensor(kl[(j - KQ) % 2][:, :], kf[(j - KQ) % 2][:, :], kh[(j - KQ) % 2][:, :],
                                            ALU.subtract).then_inc(g["kl"], 1)
                if there(b, BATCH):
                    with apart(pool, 2 * b + 2) as count:
                        if due(b - 3):
                            pool.wait_ge(p["num"], b - 3)
                        pool.wait_ge(a["eq"], 1)
                        pool.wait_ge(a["eq"], count)
                    nc.gpsimd.tensor_tensor(ql[(j - KQ) % 4][:, QD:HH, 0:S], qf[(j - KQ) % 2][:, QD:HH, :],
                                            qh[(j - KQ) % 4][:, QD:HH, 0:S], ALU.subtract).then_inc(g["ql"], 1)
            pipeline(pool, step, BATCH, 4, PR, peel=PR + 1)


@with_exitstack_sb
def ffn(nc, sb, sem, bank, ins, out, v):
    fp32, bf16 = mybir.dt.float32, mybir.dt.bfloat16
    ALU, ACT, AX = mybir.AluOpType, mybir.ActivationFunctionType, mybir.AxisListType.X
    ident, identb, causalb, neg_half = v["ident"], v["identb"], v["causalb"], v["neg_half"]
    f_wh, f_wl, f_bqk, f_bparts, f_wp, f_wg2, f_cw, f_cb = (
        v[n] for n in ("f_wh", "f_wl", "f_bqk", "f_bparts", "f_wp", "f_wg2", "f_cw", "f_cb"))
    h_all, ones, onesb, f32r = v["h_all"], v["ones"], v["onesb"], mybir.dt.float32r
    V1 = HD + 1
    SCALE = HD ** -0.5

    stats = [sb(f"f_stats{i}", [S, 6]) for i in range(2)]
    mv = [sb(f"f_mv{i}", [S, 2]) for i in range(2)]
    vare = [sb(f"f_vare{i}", [S, 1]) for i in range(2)]
    rstd = [sb(f"f_rstd{i}", [S, 1]) for i in range(2)]
    z = [sb(f"f_z{i}", [S, DIM]) for i in range(2)]
    zTh = [sb(f"f_zTh{i}", [128, 2, G, SP], f32r) for i in range(2)]
    zTl = [sb(f"f_zTl{i}", [128, G, SP], f32r) for i in range(2)]
    hid = [sb(f"f_hid{i}", [S, G, NH + 1]) for i in range(2)]
    gprod = sb("f_gprod", [S, G, NE, NH + 1])
    logit = sb("f_logit", [S, G, NE])
    q0 = [sb(f"f_q0{i}", [HD, G, S + 2]) for i in range(2)]
    q0c = [sb(f"f_q0c{i}", [128, G, S]) for i in range(2)]
    q1 = [sb(f"f_q1{i}", [128, G, S]) for i in range(2)]
    k01 = [sb(f"f_k01{i}", [128, G, S]) for i in range(2)]
    qk2 = [sb(f"f_qk2{i}", [128, G, S]) for i in range(2)]
    k2 = [sb(f"f_k2{i}", [128, G, S]) for i in range(2)]
    vv = [sb(f"f_v{i}", [S, NE, V1]) for i in range(8)]
    smax = [sb(f"f_smax{i}", [S, NE]) for i in range(2)]
    prob = [sb(f"f_prob{i}", [S, NE, S]) for i in range(2)]
    probT = [sb(f"f_probT{i}", [S, NE, S]) for i in range(2)]
    rden = [sb(f"f_rden{i}", [S, NE]) for i in range(2)]
    mixw = [sb(f"f_mixw{i}", [S, NE]) for i in range(2)]
    mixed = [sb(f"f_mixed{i}", [S, DIM]) for i in range(2)]
    mixT = [sb(f"f_mixT{i}", [KT + 1, 2, S]) for i in range(2)]
    lmax, lexp, lsum, lrec = sb("f_lmax", [S, G]), sb("f_lexp", [S, G, NE]), sb("f_lsum", [S, G]), sb("f_lrec", [S, G])
    gate, gexp = sb("f_gate", [S, G, NE]), sb("f_gexp", [S, G, NE])
    less, both, keep = sb("f_less", [S, G, 3]), sb("f_both", [S, G]), sb("f_keep", [S, G, NE])
    drop = sb("f_drop", [S, G, 2])
    gsum, grec = sb("f_gsum", [S, G]), sb("f_grec", [S, G])
    top = [sb(f"f_top{i}", [S, G, NE]) for i in range(2)]

    p = {n: sem(f"fp_{n}") for n in ("zT", "tile", "v", "score", "probT", "mix", "mixT", "out")}
    a = {n: sem(f"fa_{n}") for n in ("zT", "tile", "v", "hid", "lexp", "prob", "gexp", "probT", "mixT")}
    d = {n: sem(f"fd_{n}") for n in ("stat", "aggr", "var", "z", "zT", "logit", "conv", "smax", "prob", "lmax", "lsub", "lsum", "lrec",
                                     "gsum", "grec", "top", "rden", "mixw", "mix", "out")}
    g = {n: sem(f"fg_{n}") for n in ("set", "rstd", "prod", "gate", "shift", "less", "keep", "kept")}
    stored = sem("stored")
    B_ZT, B_TILE, B_V, B_S, B_PT, B_MIX, B_OUT = bank[0], bank[1:3], bank[3], bank[4], bank[5], bank[6], bank[7]
    ZS, ZT, TL, VS, LG, CV, SC, PT, MX, MT, OT = 1, 2, 6, 6, 10, 7, 11, 12, 13, 14, 14
    N_SET = 22
    PASSES = [(0, f_wh, 0), (0, f_wl, 0), (2, f_wh, 0), (1, f_wh, 1), (1, f_wl, 1)]

    def zpart(n, u, s=slice(None)):
        return zTl[u][:, s] if n == 2 else zTh[u][:, n, s]

    def col(x):
        return x.rearrange("p (b n) -> p b n", n=1)

    with nc.Block() as block:
        @block.sync
        def _(sp):
            def step(t, j, i):
                b = t - OT
                if there(b, BATCH):
                    sp.wait_ge(d["out"], b + 1)
                    sp.dma_start(out[b, :, :], h_all[:, b, 0:DIM]).then_inc(stored, 16)
            pipeline(sp, step, BATCH, 8, OT)
            sp.wait_ge(stored, 16 * BATCH)

        @block.tensor
        def _(pe):
            pe.wait_ge(g["set"], N_SET)

            def step(t, j, i):
                b = t - ZT
                if there(b, BATCH):
                    pe.wait_ge(d["z"], b + 1)
                    if due(b):
                        pe.wait_ge(d["zT"], b)
                    for n in range(2):
                        last = nc.tensor.transpose(B_ZT[:, n * S:(n + 1) * S], z[(j - ZT) % 2][:, n * 64:n * 64 + 128],
                                                   ident[0:S, 0:S])
                    last.then_inc(p["zT"], 1)
                b = t - SC
                if there(b, BATCH):
                    u, s = (j - SC) % 8 // 4, (j - SC) % 4
                    pe.wait_ge(a["tile"], 3 * groups(i, j, SC) + 3)
                    pe.wait_ge(d["conv"], 3 * groups(i, j, SC) + 3)
                    if due(b):
                        pe.wait_ge(d["prob"], b)
                    nc.tensor.matmul(B_S[0:S, 0:NE * S], identb[0:S, 0:S], causalb[:, :, :].rearrange("p e s -> p (e s)"),
                                     start=True, stop=False, skip_group_check=True)
                    for e, (ql, kr) in enumerate([(q0c[u], k01[u]), (q1[u], k01[u]), (qk2[u], k2[u])]):
                        last = nc.tensor.matmul(B_S[0:S, e * S:(e + 1) * S], ql[:, s, :], kr[:, s, :], start=False, stop=(e == NE - 1),
                                                skip_group_check=True)
                    last.then_inc(p["score"], 1)
                b = t - TL
                n = (j - TL) % 4
                if n < 3 and there(b, BATCH):
                    u, c = (j - TL) % 8 // 4, groups(i, j, TL)
                    pe.wait_ge(d["zT"], 4 * c + 4)
                    if due(3 * c + n - 1):
                        pe.wait_ge(a["tile"], 3 * c + n - 1)
                    for k, (x, w, r) in enumerate(PASSES):
                        last = nc.tensor.matmul(B_TILE[n % 2][:, 0:G * SP], w[:, r, n * 128:(n + 1) * 128],
                                                zpart(x, u).rearrange("p b s -> p (b s)"),
                                                start=(k == 0), stop=(k == len(PASSES) - 1))
                    last.then_inc(p["tile"], 1)
                b = t - VS
                if there(b, BATCH):
                    u, s = (j - VS) % 8 // 4, (j - VS) % 4
                    if due(b):
                        pe.wait_ge(a["hid"], b)
                    nc.tensor.matmul(B_V[:, 0:DIM + NH], onesb[0:3, :], f_bparts[:, :], start=True, stop=False)
                    pe.wait_ge(d["zT"], b + 1)
                    for k, (x, w, r) in enumerate(PASSES):
                        last = nc.tensor.matmul(B_V[0:S, 0:DIM + NH], zpart(x, u, s)[:, 0:S], w[:, r, 2 * DIM:FW],
                                                start=False, stop=(k == len(PASSES) - 1))
                    last.then_inc(p["v"], 1)
                b = t - MT
                if there(b, BATCH):
                    pe.wait_ge(d["mix"], b + 1)
                    if due(b):
                        pe.wait_ge(d["out"], b)
                    for n in range(2):
                        last = nc.tensor.transpose(B_OUT[0:KT, n * S:(n + 1) * S], mixed[(j - MT) % 2][:, n * KT:(n + 1) * KT],
                                                   ident[0:S, 0:S])
                    last.then_inc(p["mixT"], 1)
                b = t - PT
                if there(b, BATCH):
                    pe.wait_ge(a["prob"], b + 1)
                    if due(b):
                        pe.wait_ge(a["probT"], b)
                    for e in range(NE):
                        last = nc.tensor.transpose(B_PT[0:S, e * S:(e + 1) * S], prob[(j - PT) % 2][:, e, :], ident[0:S, 0:S])
                    last.then_inc(p["probT"], 1)
                b = t - MX
                if there(b, BATCH):
                    pe.wait_ge(a["probT"], b + 1)
                    pe.wait_ge(a["v"], b + 1)
                    if due(b):
                        pe.wait_ge(d["mix"], b)
                    for e in range(NE):
                        last = nc.tensor.matmul(B_MIX[0:S, e * V1:(e + 1) * V1], probT[(j - MX) % 2][:, e, :],
                                                vv[(j - MX) % 8][:, e, :], start=True, stop=True)
                    last.then_inc(p["mix"], 1)
                b = t - OT
                if there(b, BATCH):
                    pe.wait_ge(a["mixT"], b + 1)
                    for n in range(2):
                        last = nc.tensor.matmul(B_OUT[0:S, 0:DIM], mixT[(j - OT) % 2][0:KT + n, n, :], f_wp[0:KT + n, n, :],
                                                start=(n == 0), stop=(n == 1))
                    last.then_inc(p["out"], 1)
            pipeline(pe, step, BATCH, 8, OT)

        @block.scalar
        def _(act):
            act.wait_ge(g["set"], N_SET)

            def step(t, j, i):
                b = t - MX
                if there(b, BATCH):
                    act.wait_ge(p["probT"], b + 1)
                    if due(b - 1):
                        act.wait_ge(p["mix"], b - 1)
                    nc.scalar.activation(probT[(j - MX) % 2][:, :, :], B_PT[0:S, 0:NE * S].rearrange("p (e s) -> p e s", e=NE),
                                         ACT.Copy).then_inc(a["probT"], 1)
                b = t - ZT
                if there(b, BATCH):
                    u, s = (j - ZT) % 8 // 4, (j - ZT) % 4
                    act.wait_ge(p["zT"], b + 1)
                    if due(b - 7):
                        act.wait_ge(p["v"], b - 7)
                    if s == 0:
                        if due(3 * groups(i, j, ZT) - 3):
                            act.wait_ge(p["tile"], 3 * groups(i, j, ZT) - 3)
                    nc.scalar.activation(zTh[u][:, :, s, 0:S], B_ZT[:, 0:2 * S].rearrange("p (n s) -> p n s", n=2),
                                         ACT.Copy).then_inc(a["zT"], 1)
                b = t - MT
                if there(b, BATCH):
                    act.wait_ge(p["mixT"], b + 1)
                    if due(b - 1):
                        act.wait_ge(p["out"], b - 1)
                    nc.scalar.activation(mixT[(j - MT) % 2][0:KT, :, :], B_OUT[0:KT, 0:2 * S].rearrange("p (n s) -> p n s", n=2),
                                         ACT.Copy).then_inc(a["mixT"], 1)
                b = t - TL
                n = (j - TL) % 4
                if n < 3 and there(b, BATCH):
                    u, c = (j - TL) % 8 // 4, groups(i, j, TL)
                    act.wait_ge(p["tile"], 3 * c + n + 1)
                    src = B_TILE[n % 2][:, 0:G * SP].rearrange("p (b s) -> p b s", b=G)[:, :, 0:S]
                    bias = f_bqk[:, n:n + 1]
                    if n == 0:
                        if due(4 * c - 4):
                            act.wait_ge(p["score"], 4 * c - 4)
                        nc.scalar.activation(q1[u][HD:128, :, :], src[HD:128], ACT.Identity, bias=bias[HD:128])
                        nc.scalar.activation(q0[u][:, :, 1:S + 1], src[0:HD], ACT.Identity, bias=bias[0:HD]).then_inc(a["tile"], 1)
                    elif n == 1:
                        nc.scalar.activation(k01[u][:, :, :], src, ACT.Identity, bias=bias).then_inc(a["tile"], 1)
                    else:
                        nc.scalar.activation(qk2[u][:, :, :], src, ACT.Identity, bias=bias)
                        nc.scalar.activation(k2[u][0:HD, :, :], src[HD:128], ACT.Identity, bias=bias[HD:128]).then_inc(a["tile"], 1)
                b = t - SC
                if there(b, BATCH):
                    act.wait_ge(d["prob"], b + 1)
                    x = prob[(j - SC) % 2]
                    nc.scalar.activation(x[:, :, :], x[:, :, :], ACT.Exp, scale=SCALE).then_inc(a["prob"], 1)
                b = t - VS
                if there(b, BATCH):
                    u, s = (j - VS) % 8 // 4, (j - VS) % 4
                    act.wait_ge(p["v"], b + 1)
                    if due(b - 7):
                        act.wait_ge(p["mix"], b - 7)
                    nc.scalar.activation(vv[(j - VS) % 8][:, :, 0:HD], B_V[0:S, 0:DIM].rearrange("p (e d) -> p e d", e=NE),
                                         ACT.Copy).then_inc(a["v"], 1)
                    if due(groups(i, j, VS) - 1):
                        act.wait_ge(g["prod"], groups(i, j, VS) - 1)
                    nc.scalar.activation(hid[u][:, s, 0:NH], B_V[0:S, DIM:DIM + NH], ACT.Relu).then_inc(a["hid"], 1)
                b = t - LG
                if (j - LG) % 4 == 0 and there(b, BATCH):
                    act.wait_ge(d["lsub"], groups(i, j, LG) + 1)
                    nc.scalar.activation(lexp[:, :, :], lexp[:, :, :], ACT.Exp).then_inc(a["lexp"], 1)
                b = t - LG - 2
                if (j - LG - 2) % 4 == 0 and there(b, BATCH):
                    act.wait_ge(g["shift"], groups(i, j, LG + 2) + 1)
                    nc.scalar.activation(gexp[:, :, :], gexp[:, :, :], ACT.Exp).then_inc(a["gexp"], 1)
            pipeline(act, step, BATCH, 8, OT)

        @block.vector
        def _(dve):
            dve.wait_ge(g["set"], N_SET)
            for i in range(2):
                pad = zTh[i][:, :, :, S:SP]
                nc.vector.tensor_copy(pad, ones[:, 0:2 * G].rearrange("p (n b s) -> p n b s", n=2, b=G))
                nc.vector.tensor_copy(zTl[i][:, :, S:SP], ones[:, 0:G].rearrange("p (b s) -> p b s", b=G))

            def step(t, j, i):
                m, n, r = t - MT, t - ZT, t - SC
                um, un, ur, u = (j - MT) % 2, (j - ZT) % 8 // 4, (j - SC) % 2, j % 2
                mix = B_MIX[0:S, 0:NE * V1].rearrange("p (e d) -> p e d", e=NE)
                if there(m, BATCH):
                    dve.wait_ge(p["mix"], m + 1)
                    nc.vector.reciprocal(rden[um][:, :], mix[:, :, HD]).then_inc(d["rden"], 1)
                if there(t, BATCH):
                    nc.vector.bn_stats(stats[u][:, :], h_all[:, t, 0:DIM]).then_inc(d["stat"], 1)
                if there(m, BATCH):
                    dve.wait_ge(d["rden"], m + 1)
                    dve.wait_ge(d["top"], groups(i, j, MT) + 1)
                    nc.vector.tensor_tensor(mixw[um][:, :], rden[um][:, :], top[(j - MT) % 8 // 4][:, (j - MT) % 4, :],
                                            ALU.mult).then_inc(d["mixw"], 1)
                if there(n, BATCH):
                    s = (j - ZT) % 4
                    dve.wait_ge(a["zT"], n + 1)
                    nc.vector.tensor_tensor(zTh[un][0:64, 1, s, 0:S], B_ZT[64:128, S:2 * S], zTh[un][64:128, 1, s, 0:S],
                                            ALU.subtract)
                if there(m, BATCH):
                    if due(m - 1):
                        dve.wait_ge(p["mixT"], m - 1)
                    dve.wait_ge(d["mixw"], m + 1)
                    nc.vector.tensor_tensor(mixed[um][:, :].rearrange("p (e d) -> p e d", e=NE), mix[:, :, 0:HD],
                                            mixw[um][:, :].rearrange("p (e n) -> p e n", n=1).broadcast_to([S, NE, HD]),
                                            ALU.mult).then_inc(d["mix"], 1)
                if there(n, BATCH):
                    nc.vector.tensor_tensor(zTl[un][:, s, 0:S], B_ZT[:, 0:S], zTh[un][:, 0, s, 0:S],
                                            ALU.subtract).then_inc(d["zT"], 1)
                if there(t, BATCH):
                    with apart(dve, t + 1) as count:
                        dve.wait_ge(d["stat"], 1)
                        dve.wait_ge(d["stat"], count)
                    nc.vector.bn_aggr(mv[u][:, :], stats[u][:, :]).then_inc(d["aggr"], 1)
                if there(r, BATCH):
                    src = B_S[0:S, 0:NE * S].rearrange("p (e s) -> p e s", e=NE)
                    dve.wait_ge(p["score"], r + 1)
                    nc.vector.reduce_max(smax[ur][:, :], src, AX).then_inc(d["smax"], 1)
                if there(t, BATCH):
                    if due(t - 1):
                        dve.wait_ge(g["rstd"], t - 1)
                    dve.wait_ge(d["aggr"], t + 1)
                    nc.vector.tensor_scalar(vare[u][:, :], mv[u][:, 1:2], LN_EPS, None, ALU.add).then_inc(d["var"], 1)
                if there(r, BATCH):
                    if due(r - 1):
                        dve.wait_ge(p["probT"], r - 1)
                    dve.wait_ge(d["smax"], r + 1)
                    nc.vector.tensor_tensor(prob[ur][:, :, :], src,
                                            smax[ur][:, :].rearrange("p (e n) -> p e n", n=1).broadcast_to([S, NE, S]),
                                            ALU.subtract).then_inc(d["prob"], 1)
                b = t - ZS
                if there(b, BATCH):
                    u = (j - ZS) % 2
                    dve.wait_ge(g["rstd"], b + 1)
                    if due(b - 1):
                        dve.wait_ge(p["zT"], b - 1)
                    nc.vector.tensor_scalar(z[u][:, :], h_all[:, b, 0:DIM], mv[u][:, 0:1], rstd[u][:, 0:1],
                                            ALU.subtract, ALU.mult).then_inc(d["z"], 1)
                b = t - CV
                if (j - CV) % 4 == 0 and there(b, BATCH):
                    u, c = (j - CV) % 8 // 4, groups(i, j, CV)
                    x, y = q0[u][:, :, :], q0c[u][0:HD, :, :]
                    dve.wait_ge(a["tile"], 3 * c + 1)
                    if due(b - 4):
                        dve.wait_ge(p["score"], b - 4)
                    nc.vector.tensor_scalar(y, x[:, :, 1:S + 1], f_cw[:, 1:2], f_cb[:, 0:1], ALU.mult, ALU.add)\
                        .then_inc(d["conv"], 1)
                    dve.wait_ge(d["conv"], 3 * c + 1)
                    nc.vector.scalar_tensor_tensor(y, x[:, :, 0:S], f_cw[:, 0:1], y,
                                                   ALU.mult, ALU.add).then_inc(d["conv"], 1)
                    dve.wait_ge(d["conv"], 3 * c + 2)
                    nc.vector.scalar_tensor_tensor(y, x[:, :, 2:S + 2], f_cw[:, 2:3], y,
                                                   ALU.mult, ALU.add).then_inc(d["conv"], 1)
                b = t - LG
                if (j - LG) % 4 == 0 and there(b, BATCH):
                    c = groups(i, j, LG)
                    dve.wait_ge(g["prod"], c + 1)
                    nc.vector.reduce_sum(logit[:, :, :], gprod[:, :, :, :], AX).then_inc(d["logit"], 1)
                    dve.wait_ge(d["logit"], c + 1)
                    nc.vector.reduce_max(lmax[:, :], logit[:, :, :], AX).then_inc(d["lmax"], 1)
                    dve.wait_ge(d["lmax"], c + 1)
                    if due(c):
                        dve.wait_ge(g["gate"], c)
                    nc.vector.tensor_tensor(lexp[:, :, :], logit[:, :, :], col(lmax[:, :]).broadcast_to([S, G, NE]), ALU.subtract)\
                        .then_inc(d["lsub"], 1)
                b = t - LG - 1
                if (j - LG - 1) % 4 == 0 and there(b, BATCH):
                    c = groups(i, j, LG + 1)
                    dve.wait_ge(a["lexp"], c + 1)
                    nc.vector.reduce_sum(lsum[:, :], lexp[:, :, :], AX).then_inc(d["lsum"], 1)
                    dve.wait_ge(d["lsum"], c + 1)
                    if due(c):
                        dve.wait_ge(g["shift"], c)
                    nc.vector.reciprocal(lrec[:, :], lsum[:, :]).then_inc(d["lrec"], 1)
                b = t - LG - 3
                if (j - LG - 3) % 4 == 0 and there(b, BATCH):
                    c, u = groups(i, j, LG + 3), (j - LG - 3) % 8 // 4
                    dve.wait_ge(g["kept"], c + 1)
                    nc.vector.reduce_sum(gsum[:, :], keep[:, :, :], AX).then_inc(d["gsum"], 1)
                    dve.wait_ge(d["gsum"], c + 1)
                    nc.vector.reciprocal(grec[:, :], gsum[:, :]).then_inc(d["grec"], 1)
                    dve.wait_ge(d["grec"], c + 1)
                    nc.vector.tensor_tensor(top[u][:, :, :], keep[:, :, :], col(grec[:, :]).broadcast_to([S, G, NE]), ALU.mult)\
                        .then_inc(d["top"], 1)
                b = t - OT
                if there(b, BATCH):
                    dve.wait_ge(p["out"], b + 1)
                    nc.vector.tensor_tensor(h_all[:, b, 0:DIM], B_OUT[0:S, 0:DIM], h_all[:, b, 0:DIM], ALU.add)\
                        .then_inc(d["out"], 1)
            pipeline(dve, step, BATCH, 8, OT)

        @block.gpsimd
        def _(pool):
            for i in range(8):
                nc.gpsimd.memset(vv[i][:, :, HD:V1], 1.0).then_inc(g["set"], 1)
            for i in range(2):
                nc.gpsimd.memset(q0[i][:, :, 0:1], 0.0).then_inc(g["set"], 1)
                nc.gpsimd.memset(q0[i][:, :, S + 1:S + 2], 0.0).then_inc(g["set"], 1)
                nc.gpsimd.memset(q0c[i][:, :, :], 0.0).then_inc(g["set"], 1)
                nc.gpsimd.memset(q1[i][:, :, :], 0.0).then_inc(g["set"], 1)
                nc.gpsimd.memset(k2[i][:, :, :], 0.0).then_inc(g["set"], 1)
                nc.gpsimd.memset(hid[i][:, :, NH:NH + 1], 1.0).then_inc(g["set"], 1)
            pool.wait_ge(g["set"], 20)
            for i in range(2):
                nc.gpsimd.memset(mixT[i][KT:KT + 1, :, :], 1.0).then_inc(g["set"], 1)
            pool.wait_ge(g["set"], N_SET)

            def step(t, j, i):
                b = t - LG
                if (j - LG) % 4 == 0 and there(b, BATCH):
                    c, u = groups(i, j, LG), (j - LG) % 8 // 4
                    with apart(pool, b + 4) as count:
                        if due(c):
                            pool.wait_ge(d["logit"], c)
                        pool.wait_ge(a["hid"], 1)
                        pool.wait_ge(a["hid"], count)
                    nc.gpsimd.tensor_tensor(
                        gprod[:, :, :, :],
                        hid[u][:, :, :].rearrange("p b (e n) -> p b e n", e=1).broadcast_to([S, G, NE, NH + 1]),
                        f_wg2[:, :, :].rearrange("p (b e) n -> p b e n", b=1).broadcast_to([S, G, NE, NH + 1]),
                        ALU.mult).then_inc(g["prod"], 1)
                b = t
                if there(b, BATCH):
                    u = j % 2
                    if due(b - 1):
                        pool.wait_ge(d["z"], b - 1)
                    with apart(pool, b + 1) as count:
                        pool.wait_ge(d["var"], 1)
                        pool.wait_ge(d["var"], count)
                    nc.gpsimd.tensor_tensor(rstd[u][:, :], vare[u][:, :], neg_half[0:S, 0:1], ALU.pow).then_inc(g["rstd"], 1)
                b = t - LG - 1
                if (j - LG - 1) % 4 == 0 and there(b, BATCH):
                    c = groups(i, j, LG + 1)
                    with apart(pool, c + 1) as count:
                        pool.wait_ge(d["lrec"], 1)
                        pool.wait_ge(d["lrec"], count)
                    nc.gpsimd.tensor_tensor(gate[:, :, :], lexp[:, :, :], col(lrec[:, :]).broadcast_to([S, G, NE]), ALU.mult)\
                        .then_inc(g["gate"], 1)
                    with apart(pool, c + 1) as count:
                        pool.wait_ge(g["gate"], 1)
                        pool.wait_ge(g["gate"], count)
                    nc.gpsimd.tensor_tensor(gexp[:, :, :], gate[:, :, :], col(lrec[:, :]).broadcast_to([S, G, NE]), ALU.subtract)\
                        .then_inc(g["shift"], 1)
                    nc.gpsimd.tensor_tensor(less[:, :, 0:2], gate[:, :, 0:1].broadcast_to([S, G, 2]), gate[:, :, 1:3],
                                            ALU.subtract).then_inc(g["less"], 1)
                    nc.gpsimd.tensor_tensor(less[:, :, 2], gate[:, :, 1], gate[:, :, 2], ALU.subtract).then_inc(g["less"], 1)
                    with apart(pool, 6 * c + 2) as count:
                        pool.wait_ge(g["less"], 1)
                        pool.wait_ge(g["less"], count)
                    nc.gpsimd.tensor_scalar(less[:, :, :], less[:, :, :], 0.0, None, ALU.is_lt).then_inc(g["less"], 1)
                    with apart(pool, 6 * c + 3) as count:
                        pool.wait_ge(g["less"], 1)
                        pool.wait_ge(g["less"], count)
                    nc.gpsimd.tensor_tensor(drop[:, :, 0], less[:, :, 0], less[:, :, 1], ALU.mult).then_inc(g["less"], 1)
                    nc.gpsimd.tensor_tensor(both[:, :], less[:, :, 0], less[:, :, 2], ALU.mult).then_inc(g["less"], 1)
                    with apart(pool, 6 * c + 5) as count:
                        pool.wait_ge(g["less"], 1)
                        pool.wait_ge(g["less"], count)
                    nc.gpsimd.tensor_tensor(drop[:, :, 1], less[:, :, 2], both[:, :], ALU.subtract).then_inc(g["less"], 1)
                b = t - LG - 2
                if (j - LG - 2) % 4 == 0 and there(b, BATCH):
                    c = groups(i, j, LG + 2)
                    with apart(pool, 6 * c + 6) as count:
                        pool.wait_ge(g["less"], 1)
                        pool.wait_ge(g["less"], count)
                    if due(c):
                        with apart(pool, c) as count:
                            pool.wait_ge(d["top"], 1)
                            pool.wait_ge(d["top"], count)
                    nc.gpsimd.tensor_scalar(keep[:, :, 0:2], drop[:, :, :], -1.0, 1.0, ALU.mult, ALU.add).then_inc(g["keep"], 1)
                    nc.gpsimd.tensor_tensor(keep[:, :, 2], drop[:, :, 0], drop[:, :, 1], ALU.add).then_inc(g["keep"], 1)
                    pool.wait_ge(a["gexp"], c + 1)
                    with apart(pool, 2 * c + 2) as count:
                        pool.wait_ge(g["keep"], 1)
                        pool.wait_ge(g["keep"], count)
                    nc.gpsimd.tensor_tensor(keep[:, :, :], keep[:, :, :], gexp[:, :, :], ALU.mult).then_inc(g["kept"], 1)
            pipeline(pool, step, BATCH, 8, OT)


def groups(i, j, skew):
    return 2 * i + (j - skew) // 4


def kernel(**inputs):
    import numpy as np
    import concourse.bacc as _bacc
    from concourse.bass_utils import run_bass_kernel_spmd as _run

    x = {k: np.asarray(a) for k, a in inputs.items()}
    f32 = np.float32
    pre = lambda n: x["L0_" + n]
    n, k = np.arange(FRAME), np.arange(NFFT)
    window = 0.54 - 0.46 * np.cos(2.0 * np.pi * n / (FRAME - 1))
    angle = 2.0 * np.pi * np.outer(n, k) / FRAME
    dft = np.concatenate([window[:, None] * np.cos(angle), window[:, None] * np.sin(angle[:, 1:NFFT - 1])], 1)
    heads = np.tile(np.arange(HEADS)[:, None] == np.arange(HEADS * M)[None, :] // M, (3, 1)).astype(f32)
    less_q, less_k = np.zeros((KZ, 2), f32), np.zeros((KZ, 2), f32)
    for i, (_, w) in enumerate(PAIRS):
        less_q[KB + i * NY:KB + (i + 1) * NY, 0:w] = -1.0
        less_k[i * NY:(i + 1) * NY, 0:w] = -1.0
    less_e = np.zeros((KP, 2), f32)
    less_e[NMEL:2 * NMEL, 0] = -1.0
    less_e[2 * NMEL:NL, 1] = less_e[NL + 1, 1] = -1.0
    consts = {
        "less_e": less_e,
        "dft": dft.astype(f32), "ident": np.eye(128, dtype=f32), "heads": heads, "less_q": less_q, "less_k": less_k,
        "less_b": -np.tri(3, 2, -1, dtype=f32),
        "blk": (np.arange(KT)[:, None] // DH == np.arange(HH * NY)[None, :] // NY).astype(f32),
        "bd": (np.arange(128)[:, None] // M == np.arange(2)[None, :]).astype(f32),
        "causal": np.where(np.arange(S)[None, :] > np.arange(S)[:, None], NEG, 0.0).astype(f32),
    }
    mel, dct = pre("tok_mel_filters"), pre("tok_dct")
    dctx = np.zeros((NY, KP), f32)
    for i in range(3):
        dctx[0:NMFCC, i * NMEL:(i + 1) * NMEL] = dct
    dctx[NMFCC, NL:KP] = 1.0
    projb = np.zeros((KT, HH * M), f32)
    for h in range(HH):
        projb[h * DH:(h + 1) * DH, h * M:(h + 1) * M] = pre("attn_proj").T
    order = [0, 1, 3, 4, 2, 5]
    mix = lambda a: np.concatenate([a[..., i * HD:(i + 1) * HD] for i in order], -1)
    arrays = {
        **consts,
        "x": x["x"], "mel2": np.tile(np.concatenate([mel.T, mel.T[1:NFFT - 1]]), (1, 3)), "dctx": dctx, "dctxT": dctx.T,
        "wpb": np.concatenate([pre("tok_w_proj"), pre("tok_b_proj")[None]]),
        "wq": pre("attn_Wq"), "wk": pre("attn_Wk"), "wv": pre("attn_Wv"), "wo": pre("attn_Wo"), "projb": projb,
        "f_w": np.concatenate([mix(pre("ffn_Wqk")), *pre("ffn_Wv"), pre("ffn_Wg1")], 1),
        "f_bqk": mix(pre("ffn_bqk")).reshape(3, 128).T,
        "f_bvg": np.concatenate([pre("ffn_bv").reshape(DIM), pre("ffn_bg1")])[None],
        "f_wp": pre("ffn_Wp"), "f_bp": pre("ffn_bp")[None],
        "f_wg2": np.concatenate([pre("ffn_Wg2"), pre("ffn_bg2")[None]]).T.reshape(1, NE * (NH + 1)),
        "f_cw": pre("ffn_conv_w").reshape(HD, 3), "f_cb": pre("ffn_conv_b")[:, None],
    }
    nc = _bacc.Bacc("TRN2", target_bir_lowering=False, num_devices=1)
    feed, ins = {}, {}
    for name, a in arrays.items():
        a = np.ascontiguousarray(a)
        feed[f"in_{name}"] = a
        ins[name] = nc.dram_tensor(f"in_{name}", a.shape, mybir.dt.from_np(a.dtype), kind="ExternalInput").ap()
    out = nc.dram_tensor("out_0", (BATCH, S, DIM), mybir.dt.float32, kind="ExternalOutput").ap()
    audio_tower(nc, ins, out)
    r = _run(nc, [feed], core_ids=[0])
    return r.results[0]["out_0"]
```
